# Optimizing a Trainium2 kernel written in Bass

```python
import numpy as np
import jax
import jax.numpy as jnp

def _softmax(x, axis=-1):
    return jax.nn.softmax(x, axis=axis)

def _gelu(x):
    return jax.nn.gelu(x, approximate=True)

def _silu(x):
    return jax.nn.silu(x)

def _sigmoid(x):
    return jax.nn.sigmoid(x)

def _layernorm(x, axis=-1, eps=1e-05):
    m = jnp.mean(x, axis=axis, keepdims=True)
    v = jnp.var(x, axis=axis, keepdims=True)
    return (x - m) / jnp.sqrt(v + eps)

def _scatter_add(tgt, idx, src, axis=0):
    return tgt.at[idx].add(src)

def _segment_sum(src, seg, n):
    return jax.ops.segment_sum(src, seg, n)
kernel_name = 'mk_pixart_seq_d2_seqx_r4_bc50b8'

def setup_inputs(seed: int=0):
    np.random.seed(seed)
    _w = jnp.asarray

    def _rec_inputs():
        import jax
        import jax.numpy as jnp
        _rk = jax.random.key(seed)
        x = 7.22e-05 + 1 * jax.random.normal(jax.random.fold_in(_rk, 1), (16, 128, 256), jnp.float32)
        _lenS = 128 - jax.random.randint(jax.random.fold_in(_rk, 7), (16,), 0, max(1, 128 // 4) + 1, jnp.int32)
        _lenS2 = 128 - jax.random.randint(jax.random.fold_in(_rk, 8), (16,), 0, max(1, 128 // 4) + 1, jnp.int32)
        cond_1024 = 0.000887014 + 1.03683 * jax.random.normal(jax.random.fold_in(_rk, 11), (16, 256), jnp.float32)
        _ctx_1024P = jax.random.normal(jax.random.fold_in(_rk, 12), (16, 16, 256), jnp.float32)
        _ctx_1024c = jax.random.dirichlet(jax.random.fold_in(_rk, 512), 0.3 * jnp.ones((16,), jnp.float32), (16, 128))
        _ctx_1024t = jnp.einsum('bsk,bkd->bsd', _ctx_1024c, _ctx_1024P)
        _ctx_1024t = _ctx_1024t * jax.lax.rsqrt(jnp.mean(jnp.square(_ctx_1024t)) + 1e-12) * 0.953939
        ctx_1024 = 0.00086875 + 0.999764 * (_ctx_1024t + 0.3 * jax.random.normal(jax.random.fold_in(_rk, 612), (16, 128, 256), jnp.float32))
        return (x, cond_1024, ctx_1024)
    x, cond_1024, ctx_1024 = _rec_inputs()

    def _L0_xcond_setup():
        import jax, jax.numpy as jnp
        import numpy as np
        C = 256
        H = 16
        D = C // H
        WIN = 128
        SHIFT = 64
        TOPK = 16
        HID = 1024
        EPS = 1e-06

        def _ln(x):
            x32 = x.astype(jnp.float32)
            m = x32.mean(-1, keepdims=True)
            v = jnp.mean((x32 - m) ** 2, axis=-1, keepdims=True)
            return ((x32 - m) * jax.lax.rsqrt(v + EPS)).astype(x.dtype)

        def _self_attn(h, w_qkv, b_qkv, w_so, b_so):
            B, L, _ = h.shape
            qkv = h @ w_qkv + b_qkv
            qkv = jnp.roll(qkv, -SHIFT, axis=1)
            nw = L // WIN
            qkv = qkv.reshape(B, nw, WIN, 3, H, D)
            q, k, v = (qkv[:, :, :, 0], qkv[:, :, :, 1], qkv[:, :, :, 2])
            scores = jnp.einsum('bnqhd,bnkhd->bnhqk', q, k) / jnp.sqrt(jnp.float32(D)).astype(h.dtype)
            attn = jax.nn.softmax(scores, axis=-1)
            o = jnp.einsum('bnhqk,bnkhd->bnqhd', attn, v).reshape(B, L, C)
            o = jnp.roll(o, SHIFT, axis=1)
            return o @ w_so + b_so

        def _topk_cross_attn(h, ctx, w_q, b_q, w_kv, b_kv, w_co, b_co):
            B, L, _ = h.shape
            Lc = ctx.shape[1]
            q = (h @ w_q + b_q).reshape(B, L, H, D)
            kv = (ctx @ w_kv + b_kv).reshape(B, Lc, 2, H, D)
            k, v = (kv[:, :, 0], kv[:, :, 1])
            scores = jnp.einsum('bqhd,bkhd->bhqk', q, k) / jnp.sqrt(jnp.float32(D)).astype(h.dtype)
            top_s, top_i = jax.lax.top_k(scores, TOPK)
            attn = jax.nn.softmax(top_s, axis=-1)
            v_bh = jnp.transpose(v, (0, 2, 1, 3))
            vg = jnp.take_along_axis(v_bh[:, :, None, :, :], top_i[..., None], axis=3)
            o = jnp.einsum('bhqk,bhqkd->bqhd', attn, vg).reshape(B, L, C)
            return o @ w_co + b_co

        def _swiglu(h, w_m1, b_m1, w_m2, b_m2):
            u = h @ w_m1 + b_m1
            a, b = (u[..., :HID], u[..., HID:])
            return jax.nn.silu(a) * b @ w_m2 + b_m2
        key = jax.random.key(seed)
        ks = jax.random.split(key, 24)
        s = 0.02
        inp = {'x': jax.random.normal(ks[0], (2, 1024, C), jnp.float32), 'mod': jax.random.normal(ks[1], (2, C), jnp.float32), 'context': jax.random.normal(ks[2], (2, 256, C), jnp.float32), 'w_ada': jax.random.normal(ks[3], (C, 9 * C), jnp.float32) * s, 'b_ada': jnp.zeros((9 * C,), jnp.float32), 'w_qkv': jax.random.normal(ks[4], (C, 3 * C), jnp.float32) * s, 'b_qkv': jnp.zeros((3 * C,), jnp.float32), 'w_so': jax.random.normal(ks[5], (C, C), jnp.float32) * s, 'b_so': jnp.zeros((C,), jnp.float32), 'w_q': jax.random.normal(ks[6], (C, C), jnp.float32) * s, 'b_q': jnp.zeros((C,), jnp.float32), 'w_kv': jax.random.normal(ks[7], (C, 2 * C), jnp.float32) * s, 'b_kv': jnp.zeros((2 * C,), jnp.float32), 'w_co': jax.random.normal(ks[8], (C, C), jnp.float32) * s, 'b_co': jnp.zeros((C,), jnp.float32), 'w_m1': jax.random.normal(ks[9], (C, 2 * HID), jnp.float32) * s, 'b_m1': jnp.zeros((2 * HID,), jnp.float32), 'w_m2': jax.random.normal(ks[10], (HID, C), jnp.float32) * s, 'b_m2': jnp.zeros((C,), jnp.float32)}
        return inp
    _L0_xcond_all = _L0_xcond_setup()
    _L0_xcond_in = {k: v for k, v in _L0_xcond_all.items() if k in ('w_ada', 'b_ada', 'w_qkv', 'b_qkv', 'w_so', 'b_so', 'w_q', 'b_q', 'w_kv', 'b_kv', 'w_co', 'b_co', 'w_m1', 'b_m1', 'w_m2', 'b_m2')}
    del _L0_xcond_all

    def _L1_xcond_setup():
        import jax, jax.numpy as jnp
        import numpy as np
        EPS = 1e-05

        def _ada_ln(x, c, W_ss, b_ss):
            mu = jnp.mean(x, axis=-1, keepdims=True)
            var = jnp.mean((x - mu) ** 2, axis=-1, keepdims=True)
            h = (x - mu) / jnp.sqrt(var + EPS)
            ss = jax.nn.silu(c) @ W_ss + b_ss
            scale, bias = jnp.split(ss, 2, axis=-1)
            return (1.0 + scale)[:, None, :] * h + bias[:, None, :]
        key = jax.random.key(seed)
        ks = jax.random.split(key, 12)
        B, Lq, Lkv, H = (8, 512, 128, 256)
        s = 0.02
        return {'x_q': jax.random.normal(ks[0], (B, Lq, H), jnp.float32), 'x_kv': jax.random.normal(ks[1], (B, Lkv, H), jnp.float32), 't_vec': jax.random.normal(ks[2], (B, H), jnp.float32), 'Wq': jax.random.normal(ks[3], (H, H), jnp.float32) * s, 'bq': jnp.zeros((H,), jnp.float32), 'Wkv': jax.random.normal(ks[4], (H, 2 * H), jnp.float32) * s, 'bkv': jnp.zeros((2 * H,), jnp.float32), 'Wp': jax.random.normal(ks[5], (H, H), jnp.float32) * s, 'bp': jnp.zeros((H,), jnp.float32), 'Wss_q': jax.random.normal(ks[6], (H, 2 * H), jnp.float32) * s, 'bss_q': jnp.zeros((2 * H,), jnp.float32), 'Wss_kv': jax.random.normal(ks[7], (H, 2 * H), jnp.float32) * s, 'bss_kv': jnp.zeros((2 * H,), jnp.float32)}
    _L1_xcond_all = _L1_xcond_setup()
    _L1_xcond_in = {k: v for k, v in _L1_xcond_all.items() if k in ('Wq', 'bq', 'Wkv', 'bkv', 'Wp', 'bp', 'Wss_q', 'bss_q', 'Wss_kv', 'bss_kv')}
    del _L1_xcond_all
    return {'x': x, 'cond_1024': cond_1024, 'ctx_1024': ctx_1024, 'L0_xcond_w_ada': _L0_xcond_in['w_ada'], 'L0_xcond_b_ada': _L0_xcond_in['b_ada'], 'L0_xcond_w_qkv': _L0_xcond_in['w_qkv'], 'L0_xcond_b_qkv': _L0_xcond_in['b_qkv'], 'L0_xcond_w_so': _L0_xcond_in['w_so'], 'L0_xcond_b_so': _L0_xcond_in['b_so'], 'L0_xcond_w_q': _L0_xcond_in['w_q'], 'L0_xcond_b_q': _L0_xcond_in['b_q'], 'L0_xcond_w_kv': _L0_xcond_in['w_kv'], 'L0_xcond_b_kv': _L0_xcond_in['b_kv'], 'L0_xcond_w_co': _L0_xcond_in['w_co'], 'L0_xcond_b_co': _L0_xcond_in['b_co'], 'L0_xcond_w_m1': _L0_xcond_in['w_m1'], 'L0_xcond_b_m1': _L0_xcond_in['b_m1'], 'L0_xcond_w_m2': _L0_xcond_in['w_m2'], 'L0_xcond_b_m2': _L0_xcond_in['b_m2'], 'L1_xcond_Wq': _L1_xcond_in['Wq'], 'L1_xcond_bq': _L1_xcond_in['bq'], 'L1_xcond_Wkv': _L1_xcond_in['Wkv'], 'L1_xcond_bkv': _L1_xcond_in['bkv'], 'L1_xcond_Wp': _L1_xcond_in['Wp'], 'L1_xcond_bp': _L1_xcond_in['bp'], 'L1_xcond_Wss_q': _L1_xcond_in['Wss_q'], 'L1_xcond_bss_q': _L1_xcond_in['bss_q'], 'L1_xcond_Wss_kv': _L1_xcond_in['Wss_kv'], 'L1_xcond_bss_kv': _L1_xcond_in['bss_kv']}

def reference(x, cond_1024, ctx_1024, L0_xcond_w_ada, L0_xcond_b_ada, L0_xcond_w_qkv, L0_xcond_b_qkv, L0_xcond_w_so, L0_xcond_b_so, L0_xcond_w_q, L0_xcond_b_q, L0_xcond_w_kv, L0_xcond_b_kv, L0_xcond_w_co, L0_xcond_b_co, L0_xcond_w_m1, L0_xcond_b_m1, L0_xcond_w_m2, L0_xcond_b_m2, L1_xcond_Wq, L1_xcond_bq, L1_xcond_Wkv, L1_xcond_bkv, L1_xcond_Wp, L1_xcond_bp, L1_xcond_Wss_q, L1_xcond_bss_q, L1_xcond_Wss_kv, L1_xcond_bss_kv):
    import jax
    import jax.numpy as jnp

    def _L0_xcond_ref(x, mod, context, w_ada, b_ada, w_qkv, b_qkv, w_so, b_so, w_q, b_q, w_kv, b_kv, w_co, b_co, w_m1, b_m1, w_m2, b_m2):
        import jax, jax.numpy as jnp
        import numpy as np
        C = 256
        H = 16
        D = C // H
        WIN = 128
        SHIFT = 64
        TOPK = 16
        HID = 1024
        EPS = 1e-06

        def _ln(x):
            x32 = x.astype(jnp.float32)
            m = x32.mean(-1, keepdims=True)
            v = jnp.mean((x32 - m) ** 2, axis=-1, keepdims=True)
            return ((x32 - m) * jax.lax.rsqrt(v + EPS)).astype(x.dtype)

        def _self_attn(h, w_qkv, b_qkv, w_so, b_so):
            B, L, _ = h.shape
            qkv = h @ w_qkv + b_qkv
            qkv = jnp.roll(qkv, -SHIFT, axis=1)
            nw = L // WIN
            qkv = qkv.reshape(B, nw, WIN, 3, H, D)
            q, k, v = (qkv[:, :, :, 0], qkv[:, :, :, 1], qkv[:, :, :, 2])
            scores = jnp.einsum('bnqhd,bnkhd->bnhqk', q, k) / jnp.sqrt(jnp.float32(D)).astype(h.dtype)
            attn = jax.nn.softmax(scores, axis=-1)
            o = jnp.einsum('bnhqk,bnkhd->bnqhd', attn, v).reshape(B, L, C)
            o = jnp.roll(o, SHIFT, axis=1)
            return o @ w_so + b_so

        def _topk_cross_attn(h, ctx, w_q, b_q, w_kv, b_kv, w_co, b_co):
            B, L, _ = h.shape
            Lc = ctx.shape[1]
            q = (h @ w_q + b_q).reshape(B, L, H, D)
            kv = (ctx @ w_kv + b_kv).reshape(B, Lc, 2, H, D)
            k, v = (kv[:, :, 0], kv[:, :, 1])
            scores = jnp.einsum('bqhd,bkhd->bhqk', q, k) / jnp.sqrt(jnp.float32(D)).astype(h.dtype)
            top_s, top_i = jax.lax.top_k(scores, TOPK)
            attn = jax.nn.softmax(top_s, axis=-1)
            v_bh = jnp.transpose(v, (0, 2, 1, 3))
            vg = jnp.take_along_axis(v_bh[:, :, None, :, :], top_i[..., None], axis=3)
            o = jnp.einsum('bhqk,bhqkd->bqhd', attn, vg).reshape(B, L, C)
            return o @ w_co + b_co

        def _swiglu(h, w_m1, b_m1, w_m2, b_m2):
            u = h @ w_m1 + b_m1
            a, b = (u[..., :HID], u[..., HID:])
            return jax.nn.silu(a) * b @ w_m2 + b_m2
        m = jax.nn.silu(mod) @ w_ada + b_ada
        sh_msa, sc_msa, g_msa, sh_mca, sc_mca, g_mca, sh_mlp, sc_mlp, g_mlp = [m[:, i * C:(i + 1) * C][:, None, :] for i in range(9)]
        h = _ln(x) * (1 + sc_msa) + sh_msa
        h = _self_attn(h, w_qkv, b_qkv, w_so, b_so)
        x = x + h * g_msa
        h = _ln(x) * (1 + sc_mca) + sh_mca
        h = _topk_cross_attn(h, context, w_q, b_q, w_kv, b_kv, w_co, b_co)
        x = x + h * g_mca
        h = _ln(x) * (1 + sc_mlp) + sh_mlp
        h = _swiglu(h, w_m1, b_m1, w_m2, b_m2)
        x = x + h * g_mlp
        return x

    def _L1_xcond_ref(x_q, x_kv, t_vec, Wq, bq, Wkv, bkv, Wp, bp, Wss_q, bss_q, Wss_kv, bss_kv):
        import jax, jax.numpy as jnp
        import numpy as np
        EPS = 1e-05

        def _ada_ln(x, c, W_ss, b_ss):
            mu = jnp.mean(x, axis=-1, keepdims=True)
            var = jnp.mean((x - mu) ** 2, axis=-1, keepdims=True)
            h = (x - mu) / jnp.sqrt(var + EPS)
            ss = jax.nn.silu(c) @ W_ss + b_ss
            scale, bias = jnp.split(ss, 2, axis=-1)
            return (1.0 + scale)[:, None, :] * h + bias[:, None, :]
        B, Lq, H = x_q.shape
        Lkv = x_kv.shape[1]
        nh = 16
        dh = H // nh
        xq = _ada_ln(x_q, t_vec, Wss_q, bss_q)
        xkv = _ada_ln(x_kv, t_vec, Wss_kv, bss_kv)
        q = (xq @ Wq + bq).reshape(B, Lq, nh, dh)
        kv = (xkv @ Wkv + bkv).reshape(B, Lkv, 2, nh, dh)
        k = kv[:, :, 0]
        v = kv[:, :, 1]
        scores = jnp.einsum('bqhd,bkhd->bhqk', q, k) / jnp.sqrt(jnp.float32(dh))
        attn = jax.nn.softmax(scores, axis=-1)
        out = jnp.einsum('bhqk,bkhd->bqhd', attn, v).reshape(B, Lq, H)
        return x_q + (out @ Wp + bp)
    x = _L0_xcond_ref(x, cond_1024, ctx_1024, L0_xcond_w_ada, L0_xcond_b_ada, L0_xcond_w_qkv, L0_xcond_b_qkv, L0_xcond_w_so, L0_xcond_b_so, L0_xcond_w_q, L0_xcond_b_q, L0_xcond_w_kv, L0_xcond_b_kv, L0_xcond_w_co, L0_xcond_b_co, L0_xcond_w_m1, L0_xcond_b_m1, L0_xcond_w_m2, L0_xcond_b_m2)
    x = _L1_xcond_ref(x, ctx_1024, cond_1024, L1_xcond_Wq, L1_xcond_bq, L1_xcond_Wkv, L1_xcond_bkv, L1_xcond_Wp, L1_xcond_bp, L1_xcond_Wss_q, L1_xcond_bss_q, L1_xcond_Wss_kv, L1_xcond_bss_kv)
    return x

_drawn_inputs = setup_inputs


def setup_inputs(seed=0):
    import zlib

    import numpy as np

    out = dict(_drawn_inputs(seed))
    spreads = {'L0_xcond_b_ada': (0.0, 0.394),
     'L0_xcond_b_qkv': (0.0, 0.8),
     'L0_xcond_b_so': (0.0, 0.37),
     'L0_xcond_b_q': (0.0, 0.8),
     'L0_xcond_b_kv': (0.0, 0.8),
     'L0_xcond_b_co': (0.0, 0.409),
     'L0_xcond_b_m1': (0.0, 0.8),
     'L0_xcond_b_m2': (0.0, 1.404),
     'L1_xcond_bq': (0.0, 2.0),
     'L1_xcond_bkv': (0.0, 0.8),
     'L1_xcond_bp': (0.0, 0.644),
     'L1_xcond_bss_q': (0.0, 2.0),
     'L1_xcond_bss_kv': (0.0, 2.0)}
    factors = {'L0_xcond_w_qkv': 8.0,
     'L0_xcond_w_so': 6.047,
     'L0_xcond_w_q': 6.302,
     'L0_xcond_w_kv': 3.785,
     'L0_xcond_w_co': 3.47,
     'L0_xcond_w_m1': 6.149,
     'L0_xcond_w_m2': 6.14,
     'L1_xcond_Wq': 57.412,
     'L1_xcond_Wss_q': 64.0,
     'L1_xcond_Wkv': 3.922,
     'L1_xcond_Wp': 3.762,
     'L1_xcond_Wss_kv': 8.0}
    for name, (base, spread) in spreads.items():
        noise = np.random.default_rng([zlib.crc32(name.encode()), seed]).standard_normal(out[name].shape)
        drawn = base * np.exp(spread * noise) if base else spread * noise
        out[name] = jnp.asarray(drawn.astype(out[name].dtype))
    for name, factor in factors.items():
        out[name] = (out[name] * factor).astype(out[name].dtype)
    return out
```

```python
from contextlib import ExitStack

import concourse.bass as bass
from concourse import mybir

F32 = mybir.dt.float32
ALU = mybir.AluOpType
ACT = mybir.ActivationFunctionType
AX = mybir.AxisListType

P = 128
B = 16
C = 256
CK = C // P
H = 16
D = C // H
HC = P // D
HID = 1024
HB = HID // P
SLOTS = 4
ITERS = B // SLOTS
QH = 4
PHASES = 3 * SLOTS
UNITS = PHASES * (H // QH)
RING = 6
FILLS = PHASES // RING
GONE = -(2.0 ** 127)

SELF, CROSS, LAST, MLP, CTX = range(5)
LNS = {SELF: 1e-6, CROSS: 1e-6, MLP: 1e-6, LAST: 1e-5, CTX: 1e-5}
NMOD = 4 * len(LNS)
NBIAS = 18 + 4 + 4 + 4 + 2 + 2 + 2 + 2 + 16

PLAN = {}


def _put(step, *part):
    PLAN.setdefault(step, []).append(part)


for _s in range(SLOTS):
    _put(4 * _s - 3, "stats", SELF, _s)
    _put(4 * _s - 2, "norm", SELF, _s)
    _put(4 * _s - 2, "turn", SELF, _s)
    _put(4 * _s - 1, "q", SELF, _s)
    _put(4 * _s - 1, "kv", SELF, _s)
    _put(4 * _s + 4, "skip", SELF, _s)
    _put(4 * _s + 7, "out", SELF, _s)
    _put(4 * _s + 7, "stats", CROSS, _s)
    _put(4 * _s + 8, "norm", CROSS, _s)
    _put(4 * _s + 8, "turn", CROSS, _s)
    _put(4 * _s + 8, "skip", CROSS, _s)
    _put(4 * _s + 9, "q", CROSS, _s)
    _put(4 * _s + 9, "stats", CTX, _s)
    _put(4 * _s + 10, "norm", CTX, _s)
    _put(4 * _s + 11, "turn_ctx", CTX, _s)
    _put(4 * _s + 12, "kv", CROSS, _s)
    _put(4 * _s + 20, "kv", LAST, _s)
    _put(4 * _s + 23, "out", CROSS, _s)
    _put(4 * _s + 23, "stats", MLP, _s)
    _put(4 * _s + 24, "norm", MLP, _s)
    _put(4 * _s + 24, "turn", MLP, _s)
    _put(4 * _s + 24, "skip", MLP, _s)
    _put(4 * _s + 25, "up", 0, _s)
    _put(4 * _s + 26, "up", 1, _s)
    _put(4 * _s + 26, "glu", 0, _s)
    _put(4 * _s + 27, "glu", 1, _s)
    _put(4 * _s + 28, "out", MLP, _s)
    _put(4 * _s + 28, "stats", LAST, _s)
    _put(4 * _s + 29, "norm", LAST, _s)
    _put(4 * _s + 29, "turn", LAST, _s)
    _put(4 * _s + 29, "skip", LAST, _s)
    _put(4 * _s + 30, "q", LAST, _s)
    _put(4 * _s + 39, "out", LAST, _s)
FIRST_STEP, LAST_STEP = min(PLAN), max(max(PLAN), UNITS + 3)
STEPS = range(FIRST_STEP, LAST_STEP + 1)

NTH, COUNT = {}, {}
DENSE_USES = {"q": 1, "kv": 1, "turn": 1, "turn_ctx": 1, "out": 1, "up": 2}
DENSE, N_DENSE = {}, 0
for _t in sorted(PLAN):
    for _part in PLAN[_t]:
        _sort = "turn" if _part[0] == "turn_ctx" else _part[0]
        NTH[_part] = COUNT.get(_sort, 0)
        COUNT[_sort] = NTH[_part] + 1
        DENSE[_part] = N_DENSE
        N_DENSE += DENSE_USES.get(_part[0], 0)
assert N_DENSE % 2 == 0
GATE = {SELF: 0, CROSS: 1, MLP: 2}
N_OUT = COUNT["out"]
QUERY_BIAS = {SELF: 26, CROSS: 30, LAST: 34}
KEY_BIAS = {SELF: 28, CROSS: 32, LAST: 36}


def block_kernel(nc, a, out):
    with ExitStack() as ctx:
        def sb(name, *shape):
            return ctx.enter_context(nc.sbuf_tensor(name, list(shape), F32))

        def bank(name):
            return ctx.enter_context(nc.psum_tensor(name, [P, 512], F32))

        def sem(name):
            return ctx.enter_context(nc.semaphore(name))

        w_qkv = sb("w_qkv", P, CK, 3 * C)
        w_so = sb("w_so", P, CK, C)
        w_q = sb("w_q", P, CK, C)
        w_kv = sb("w_kv", P, CK, 2 * C)
        w_co = sb("w_co", P, CK, C)
        w_m1 = sb("w_m1", P, CK, 2 * HID)
        w_m2 = sb("w_m2", P, HB, C)
        l_q = sb("l_q", P, CK, C)
        l_kv = sb("l_kv", P, CK, 2 * C)
        l_p = sb("l_p", P, CK, C)
        w_query = {SELF: w_qkv[:, :, 0:C], CROSS: w_q[:], LAST: l_q[:]}
        w_key = {SELF: w_qkv[:, :, C:2 * C], CROSS: w_kv[:, :, 0:C], LAST: l_kv[:, :, 0:C]}
        w_value = {SELF: w_qkv[:, :, 2 * C:3 * C], CROSS: w_kv[:, :, C:2 * C], LAST: l_kv[:, :, C:2 * C]}
        w_out = {SELF: w_so, CROSS: w_co, LAST: l_p}
        b_value = sb("b_value", P, 3, C)
        b_out = sb("b_out", P, 4, C)
        bias_rows = sb("bias_rows", NBIAS, P)
        bias_cols = sb("bias_cols", P, NBIAS)
        mod_bias = sb("mod_bias", P, NMOD)
        silu_t = sb("silu_t", P, CK, B)
        mod_all = sb("mod_all", P, B, NMOD)
        mod_now = sb("mod_now", P, SLOTS, NMOD)
        gate_rows = sb("gate_rows", B, 3 * C)
        ident = sb("ident", P, P)
        minus_half = sb("minus_half", P, 1)
        one_cols = sb("one_cols", P, 2, 32)
        x_in = sb("x_in", P, SLOTS, C)
        ctx_in = sb("ctx_in", P, SLOTS, C)
        gates = sb("gates", P, SLOTS, 3 * C)
        x_mid = sb("x_mid", P, SLOTS, C)
        x_skip = sb("x_skip", P, SLOTS, C)
        gated = sb("gated", P, C)
        x_norm = sb("x_norm", P, 3, C)
        ln_stats = sb("ln_stats", P, 4, 6)
        ln_mv = sb("ln_mv", P, 4, 2)
        ln_var = sb("ln_var", P, 4, 1)
        ln_rstd = sb("ln_rstd", P, 4, 1)
        h_t = sb("h_t", P, SLOTS, CK, P)
        ctx_t = sb("ctx_t", P, 1, CK, P)
        ctx_norm_t = sb("ctx_norm_t", P, 3, CK, P)
        q_t = sb("q_t", P, RING, CK, P)
        k_t = sb("k_t", P, 3, CK, P)
        k_blocks = sb("k_blocks", P, RING, CK, HC, P)
        v_pad = sb("v_pad", P, RING, H // 2, 2, 32)
        neg_max = sb("neg_max", P, 4, QH)
        probs = sb("probs", P, 3, QH, P)
        left = sb("left", P, 3, QH, P)
        top8 = sb("top8", P, 2, QH, 8)
        probs_t = sb("probs_t", P, 3, QH, P)
        inv_sum = sb("inv_sum", P, CK, P)
        o_t = sb("o_t", P, CK, P)
        half_a = sb("half_a", P, 2, 4, P)
        tanh_a = sb("tanh_a", P, 2, 4, P)
        lin_b = sb("lin_b", P, 2, 4, P)
        glu = sb("glu", P, HB, P)
        gates_dram = nc.dram_tensor("gates_dram", (B, 3 * C), F32).ap()
        arena = k_blocks[:].rearrange("p r c h t -> p (r c h t)")
        NADA = 9 * C
        w_ada = arena[:, 0:CK * NADA].rearrange("p (c n) -> p c n", c=CK)
        ss_q = arena[:, CK * NADA:CK * (NADA + 2 * C)].rearrange("p (c n) -> p c n", c=CK)
        ss_kv = arena[:, CK * (NADA + 2 * C):CK * (NADA + 4 * C)].rearrange("p (c n) -> p c n", c=CK)

        spare = arena[0:B, CK * (NADA + 4 * C):]
        gate_bias = spare[:, 0:3 * C]
        cond, cond_tanh, cond_silu = (spare[:, n * C:(n + 1) * C] for n in (3, 4, 5))

        score_bank = [bank(f"score_bank{n}") for n in range(3)]
        turn_bank = [bank(f"turn_bank{n}") for n in range(2)]
        o_bank = bank("o_bank")
        dense_bank = [bank(f"dense_bank{n}") for n in range(2)]
        o_view = o_bank[:].rearrange("p (c k t) -> p c k t", c=CK, k=2)

        cond_loaded = sem("cond_loaded")
        ada_loaded = sem("ada_loaded")
        rows_loaded = sem("rows_loaded")
        bcast_loaded = sem("bcast_loaded")
        gate_bias_loaded = sem("gate_bias_loaded")
        w_loaded = {k: sem(f"w_loaded_{k}") for k in ("qkv", "so", "q", "kv", "co", "m1", "m2", "lq", "lkv", "lp")}
        x_loaded = [sem(f"x_loaded{s}") for s in range(SLOTS)]
        ctx_loaded = [sem(f"ctx_loaded{s}") for s in range(SLOTS)]
        gates_loaded = [sem(f"gates_loaded{s}") for s in range(SLOTS)]
        gates_stored = sem("gates_stored")
        k_placed = [sem(f"k_placed{r}") for r in range(RING)]
        y_stored = sem("y_stored")
        ident_step = sem("ident_step")
        consts_ready = sem("consts_ready")
        blocks_zeroed = sem("blocks_zeroed")
        w_scaled = sem("w_scaled")
        setup_act = sem("setup_act")
        setup_dve = sem("setup_dve")
        setup_pe = sem("setup_pe")
        dve_passed = sem("dve_passed")
        pool_passed = sem("pool_passed")
        sp_passed = sem("sp_passed")
        mod_ready = sem("mod_ready")
        bn_done = sem("bn_done")
        stats_done = sem("stats_done")
        var_done = sem("var_done")
        rstd_done = sem("rstd_done")
        norm_done = sem("norm_done")
        h_ready = sem("h_ready")
        q_ready = sem("q_ready")
        k_ready = sem("k_ready")
        v_ready = sem("v_ready")
        skip_part = sem("skip_part")
        skip_ready = sem("skip_ready")
        gated_done = sem("gated_done")
        x_done = sem("x_done")
        half_a_done = sem("half_a_done")
        tanh_done = sem("tanh_done")
        lin_b_done = sem("lin_b_done")
        silu_done = sem("silu_done")
        glu_done = sem("glu_done")
        dense_ready = sem("dense_ready")
        dense_free = [sem(f"dense_free{n}") for n in range(2)]
        scores_ready = sem("scores_ready")
        topk_step = sem("topk_step")
        scored = sem("scored")
        left_ready = sem("left_ready")
        probs_ready = sem("probs_ready")
        mask_done = sem("mask_done")
        top_ready = sem("top_ready")
        turned = sem("turned")
        probs_t_ready = sem("probs_t_ready")
        o_ready = sem("o_ready")
        inv_done = sem("inv_done")
        o_t_ready = sem("o_t_ready")

        block = ctx.enter_context(nc.Block())

        def phase_of(kind, s):
            return SLOTS * kind + s

        @block.sync
        def _(sp):
            def chunks(w):
                return w.rearrange("(c p) n -> p c n", p=P)

            def rows(v):
                return v.rearrange("(c p) -> c p", p=P)

            sp.dma_start(cond, a["cond_1024"]).then_inc(cond_loaded, 16)
            at = 0
            for v in (a["L0_xcond_b_ada"], a["L1_xcond_bss_q"], a["L1_xcond_bss_kv"],
                      a["L0_xcond_b_qkv"][0:2 * C], a["L0_xcond_b_q"], a["L0_xcond_b_kv"][0:C],
                      a["L1_xcond_bq"], a["L1_xcond_bkv"][0:C], a["L0_xcond_b_m1"]):
                n = v.shape[0] // P
                sp.dma_start(bias_rows[at:at + n, :], rows(v)).then_inc(rows_loaded, 16)
                at += n
            sp.dma_start(w_ada, chunks(a["L0_xcond_w_ada"])).then_inc(ada_loaded, 16)
            sp.dma_start(ss_q, chunks(a["L1_xcond_Wss_q"])).then_inc(ada_loaded, 16)
            sp.dma_start(ss_kv, chunks(a["L1_xcond_Wss_kv"])).then_inc(ada_loaded, 16)
            gate_chunks = a["L0_xcond_b_ada"].rearrange("(k n) -> k n", n=C)[2::3]
            sp.dma_start(gate_bias.rearrange("b (k n) -> b k n", n=C),
                         gate_chunks.partition_broadcast(B)).then_inc(gate_bias_loaded, 16)
            for s in range(SLOTS):
                sp.dma_start(x_in[:, s, :], a["x"][s]).then_inc(x_loaded[s], 16)
                sp.dma_start(ctx_in[:, s, :], a["ctx_1024"][s]).then_inc(ctx_loaded[s], 16)
            for key, dst, src in (("qkv", w_qkv, "L0_xcond_w_qkv"), ("q", w_q, "L0_xcond_w_q")):
                sp.dma_start(dst[:], chunks(a[src])).then_inc(w_loaded[key], 16)
            for n, v in enumerate((a["L0_xcond_b_qkv"][2 * C:3 * C], a["L0_xcond_b_kv"][C:2 * C],
                                   a["L1_xcond_bkv"][C:2 * C])):
                sp.dma_start(b_value[:, n, :], v.partition_broadcast(P)).then_inc(bcast_loaded, 16)
            for n, v in enumerate((a["L0_xcond_b_so"], a["L0_xcond_b_co"], a["L1_xcond_bp"],
                                   a["L0_xcond_b_m2"])):
                sp.dma_start(b_out[:, n, :], v.partition_broadcast(P)).then_inc(bcast_loaded, 16)
            for key, dst, src in (("so", w_so, "L0_xcond_w_so"), ("kv", w_kv, "L0_xcond_w_kv"),
                                  ("co", w_co, "L0_xcond_w_co"), ("lq", l_q, "L1_xcond_Wq"),
                                  ("lkv", l_kv, "L1_xcond_Wkv"), ("m1", w_m1, "L0_xcond_w_m1"),
                                  ("m2", w_m2, "L0_xcond_w_m2"), ("lp", l_p, "L1_xcond_Wp")):
                sp.dma_start(dst[:], chunks(a[src])).then_inc(w_loaded[key], 16)
            sp.wait_ge(setup_dve, 8)
            sp.dma_start(gates_dram, gate_rows[:]).then_inc(gates_stored, 16)
            sp.wait_ge(gates_stored, 16)
            for s in range(SLOTS):
                sp.dma_start(gates[:, s, :], gates_dram[s].partition_broadcast(P)).then_inc(gates_loaded[s], 16)
            sp.wait_ge(blocks_zeroed, 1)

            def body(i, more):
                for t in STEPS:
                    for part in PLAN.get(t, ()):
                        name, kind, s = part
                        if name == "kv":
                            r = phase_of(kind, s) % RING
                            sp.wait_ge(k_ready, i * COUNT["kv"] + NTH[part] + 1)
                            for h in range(HC):
                                rows_h = slice(D * h, D * h + D)
                                sp.dma_start(k_blocks[rows_h, r, :, h, :], k_t[rows_h, NTH[part] % 3]).then_inc(k_placed[r], 16)
                        if name == "out" and kind == LAST:
                            sp.wait_ge(x_done, i * N_OUT + NTH[part] + 1)
                            sp.sem_inc(sp_passed, 1)
                            sp.dma_start(out[i * SLOTS + s], x_mid[:, s, :]).then_inc(y_stored, 16)
                            if more:
                                nxt = (i + 1) * SLOTS + s
                                sp.dma_start(x_in[:, s, :], a["x"][nxt]).then_inc(x_loaded[s], 16)
                                sp.dma_start(ctx_in[:, s, :], a["ctx_1024"][nxt]).then_inc(ctx_loaded[s], 16)
                                sp.dma_start(gates[:, s, :], gates_dram[nxt].partition_broadcast(P)).then_inc(gates_loaded[s], 16)
                sp.wait_ge(y_stored, (i + 1) * 16 * SLOTS)
                sp.sem_inc(sp_passed, 1)

            with sp.Fori(0, ITERS - 1) as i:
                body(i, True)
            body(ITERS - 1, False)

        @block.gpsimd
        def _(pool):
            nc.gpsimd.memset(ident[:], 0.0).then_inc(ident_step, 1)
            pool.wait_ge(ident_step, 1)
            nc.gpsimd.affine_select(out=ident[:], in_=ident[:], compare_op=ALU.not_equal, fill=1.0,
                                    base=0, pattern=[[-1, P]], channel_multiplier=1).then_inc(consts_ready, 1)
            nc.gpsimd.memset(minus_half[:], -0.5)
            nc.gpsimd.memset(v_pad[:], 0.0)
            nc.gpsimd.memset(one_cols[:], 0.0).then_inc(ident_step, 1)
            pool.wait_ge(ident_step, 2)
            nc.gpsimd.memset(one_cols[:, 0, 0:D], 1.0)
            nc.gpsimd.memset(one_cols[:, 1, D:2 * D], 1.0).then_inc(consts_ready, 1)
            for key, w in (("qkv", w_query[SELF]), ("q", w_query[CROSS]), ("lq", w_query[LAST])):
                pool.wait_ge(w_loaded[key], 16)
                nc.gpsimd.tensor_scalar(w, w, 0.25, 1.0, ALU.mult, ALU.mult).then_inc(w_scaled, 1)
            pool.wait_ge(w_loaded["m1"], 16)
            nc.gpsimd.tensor_scalar(w_m1[:, :, 0:HID], w_m1[:, :, 0:HID], 0.5, 1.0, ALU.mult,
                                    ALU.mult).then_inc(w_scaled, 1)
            pool.wait_ge(bcast_loaded, 7 * 16)
            pool.wait_ge(consts_ready, 2)

            with pool.Fori(0, ITERS) as i:
                for t in STEPS:
                    if 0 <= t < UNITS and SLOTS * 4 <= t < 2 * SLOTS * 4:
                        n = t - SLOTS * 4
                        pool.wait_ge(left_ready, i * 4 * SLOTS + n + 1)
                        pool.sem_inc(pool_passed, 1)
                        nc.gpsimd.tensor_scalar(left[:, t % 3], left[:, t % 3], GONE, None,
                                                ALU.is_equal).then_inc(mask_done, 1)
                        pool.wait_ge(mask_done, i * 4 * SLOTS + n + 1)
                        pool.wait_ge(probs_ready, i * UNITS + t + 1)
                        nc.gpsimd.tensor_tensor(left[:, t % 3], left[:, t % 3], probs[:, t % 3],
                                                ALU.mult).then_inc(top_ready, 1)
                    for part in PLAN.get(t, ()):
                        name, kind, s = part
                        n = NTH[part]
                        if name == "stats":
                            pool.wait_ge(stats_done, i * COUNT["stats"] + n + 1)
                            pool.sem_inc(pool_passed, 1)
                            nc.gpsimd.tensor_scalar(ln_var[:, n % 4], ln_mv[:, n % 4, 1:2], LNS[kind], 1.0,
                                                    ALU.add, ALU.mult).then_inc(var_done, 1)
                            pool.wait_ge(var_done, i * COUNT["stats"] + n + 1)
                            nc.gpsimd.tensor_tensor(ln_rstd[:, n % 4], ln_var[:, n % 4], minus_half[:],
                                                    ALU.pow).then_inc(rstd_done, 1)
                        if name == "skip":
                            x_old = x_in if kind == SELF else x_mid
                            if kind == SELF:
                                pool.wait_ge(x_loaded[s], (i + 1) * 16)
                                pool.wait_ge(gates_loaded[s], (i + 1) * 16)
                            else:
                                before = {CROSS: SELF, MLP: CROSS, LAST: MLP}[kind]
                                pool.wait_ge(x_done, i * N_OUT + NTH["out", before, s] + 1)
                            bias = b_out[:, {SELF: 0, CROSS: 1, LAST: 2, MLP: 3}[kind], :]
                            if kind in GATE:
                                g = gates[:, s, GATE[kind] * C:(GATE[kind] + 1) * C]
                                nc.gpsimd.tensor_tensor(x_skip[:, s, :], bias, g, ALU.mult).then_inc(skip_part, 1)
                                m = n - sum(1 for q in PLAN_SKIPS_LAST if q < n)
                                pool.wait_ge(skip_part, i * (COUNT["skip"] - SLOTS) + m + 1)
                                bias = x_skip[:, s, :]
                            nc.gpsimd.tensor_tensor(x_skip[:, s, :], x_old[:, s, :], bias,
                                                    ALU.add).then_inc(skip_ready, 1)
                        if name == "glu":
                            pool.wait_ge(silu_done, i * COUNT["glu"] + n + 1)
                            pool.wait_ge(lin_b_done, i * COUNT["glu"] + n + 1)
                            nc.gpsimd.tensor_tensor(glu[:, 4 * kind:4 * kind + 4], tanh_a[:, n % 2],
                                                    lin_b[:, n % 2], ALU.mult).then_inc(glu_done, 1)

        @block.scalar
        def _(act):
            act.wait_ge(cond_loaded, 16)
            nc.scalar.activation(cond_tanh, cond, ACT.Tanh, scale=0.5).then_inc(setup_act, 1)
            act.wait_ge(setup_dve, 7)
            with act.Fori(0, ITERS) as i:
                act.wait_ge(mod_ready, i + 1)
                for t in STEPS:
                    if 0 <= t < UNITS:
                        act.wait_ge(scored, i * UNITS + t + 1)
                        for h in range(QH):
                            e = nc.scalar.activation(probs[:, t % 3, h], score_bank[t % 3][:, P * h:P * h + P],
                                                     ACT.Exp, bias=neg_max[:, t % 4, h:h + 1])
                        e.then_inc(probs_ready, 1)
                    if 0 <= t - 2 < UNITS:
                        u = t - 2
                        act.wait_ge(turned, i * UNITS + u + 1)
                        nc.scalar.copy(probs_t[:, u % 3].rearrange("p h t -> p (h t)"),
                                       turn_bank[u % 2][:]).then_inc(probs_t_ready, 1)
                    for part in PLAN.get(t, ()):
                        name, kind, s = part
                        n = DENSE[part]
                        if name in ("turn", "turn_ctx"):
                            act.wait_ge(dense_ready, i * N_DENSE + n + 1)
                            d = dense_bank[n % 2]
                            dst, at = (h_t[:, s], 0) if name == "turn" else (ctx_norm_t[:, s % 3], 2 * P)
                            if name == "turn_ctx":
                                nc.scalar.copy(ctx_t[:, 0].rearrange("p c t -> p (c t)"), d[:, 0:2 * P])
                            ln = {SELF: 0, CROSS: 1, MLP: 2, LAST: 3, CTX: 4}[kind]
                            for c in range(CK):
                                e = nc.scalar.activation(dst[:, c], d[:, at + P * c:at + P * c + P], ACT.Identity,
                                                         scale=mod_now[:, s, 4 * ln + c:4 * ln + c + 1],
                                                         bias=mod_now[:, s, 4 * ln + 2 + c:4 * ln + 3 + c])
                                if c == 0:
                                    e.then_inc(h_ready, 1)
                            e.then_inc(h_ready, 1)
                            act.wait_ge(h_ready, i * 2 * COUNT["turn"] + 2 * NTH[part] + 2)
                            act.sem_inc(dense_free[n % 2], 1)
                        if name == "up":
                            m = NTH[part]
                            act.wait_ge(half_a_done, i * COUNT["up"] + m + 1)
                            nc.scalar.activation(tanh_a[:, m % 2], half_a[:, m % 2], ACT.Tanh).then_inc(tanh_done, 1)
                            act.wait_ge(dense_ready, i * N_DENSE + n + 2)
                            for j in range(4):
                                col = 46 + 4 * kind + j
                                e = nc.scalar.activation(lin_b[:, m % 2, j], dense_bank[(n + 1) % 2][:, P * j:P * j + P],
                                                         ACT.Identity, bias=bias_cols[:, col:col + 1])
                            e.then_inc(lin_b_done, 1)
                            act.wait_ge(lin_b_done, i * COUNT["up"] + m + 1)
                            act.sem_inc(dense_free[(n + 1) % 2], 1)

        @block.vector
        def _(dve):
            dve.wait_ge(setup_act, 1)
            nc.vector.scalar_tensor_tensor(out=cond_silu, in0=cond_tanh, scalar=1.0, in1=cond,
                                           op0=ALU.add, op1=ALU.mult).then_inc(setup_dve, 1)
            dve.wait_ge(setup_dve, 1)
            nc.vector.tensor_scalar(cond_silu, cond_silu, 0.5, None, ALU.mult).then_inc(setup_dve, 1)
            dve.wait_ge(setup_pe, 1)
            nc.vector.tensor_copy(bias_cols[:], dense_bank[0][:, 0:NBIAS]).then_inc(setup_dve, 1)
            dve.wait_ge(setup_dve, 3)
            ada = bias_cols[:, 0:18].rearrange("p (k m) -> p k m", m=6)
            ss = bias_cols[:, 18:26].rearrange("p (k m) -> p k m", m=4)
            to_ada = mod_bias[:, 0:12].rearrange("p (k m) -> p k m", m=4)
            to_ss = mod_bias[:, 12:20].rearrange("p (k m) -> p k m", m=4)
            nc.vector.tensor_scalar(to_ada[:, :, 0:2], ada[:, :, 2:4], 1.0, None, ALU.add)
            nc.vector.tensor_scalar(to_ss[:, :, 0:2], ss[:, :, 0:2], 1.0, None, ALU.add)
            nc.vector.tensor_copy(to_ada[:, :, 2:4], ada[:, :, 0:2])
            nc.vector.tensor_copy(to_ss[:, :, 2:4], ss[:, :, 2:4])
            for kind in (SELF, CROSS, LAST):
                q = bias_cols[:, QUERY_BIAS[kind]:QUERY_BIAS[kind] + CK]
                nc.vector.tensor_scalar(q, q, 0.25, None, ALU.mult)
            nc.vector.tensor_scalar(bias_cols[:, 38:38 + HB], bias_cols[:, 38:38 + HB], 0.5, None,
                                    ALU.mult).then_inc(setup_dve, 1)
            dve.wait_ge(setup_pe, 2)
            nc.vector.tensor_copy(silu_t[:].rearrange("p c b -> p (c b)"),
                                  dense_bank[1][:, 0:CK * B]).then_inc(setup_dve, 1)
            dve.wait_ge(setup_pe, 3)
            nc.vector.tensor_tensor(mod_all[:].rearrange("p b j -> p j b"),
                                    score_bank[0][:, 0:NMOD * B].rearrange("p (j b) -> p j b", b=B),
                                    mod_bias[:].unsqueeze(2).broadcast_to([P, NMOD, B]),
                                    ALU.add).then_inc(setup_dve, 1)
            dve.wait_ge(gate_bias_loaded, 16)
            dve.wait_ge(setup_pe, 4)
            nc.vector.tensor_tensor(gate_rows[:, 0:2 * C], score_bank[1][0:B, :], gate_bias[:, 0:2 * C],
                                    ALU.add).then_inc(setup_dve, 1)
            nc.vector.tensor_tensor(gate_rows[:, 2 * C:3 * C], score_bank[2][0:B, 0:C], gate_bias[:, 2 * C:3 * C],
                                    ALU.add).then_inc(setup_dve, 1)
            dve.wait_ge(setup_dve, 8)
            nc.vector.memset(k_blocks[:, 0:3], 0.0)
            nc.vector.memset(k_blocks[:, 3:6], 0.0).then_inc(blocks_zeroed, 1)
            dve.wait_ge(bcast_loaded, 7 * 16)
            dve.sem_inc(dense_free[0], 1)
            dve.sem_inc(dense_free[1], 1)

            def top_k(i, u):
                n = u - 4 * SLOTS
                bank_u, l, r = score_bank[u % 3], left[:, u % 3], n % 1
                base = (i * 4 * SLOTS + n) * 4
                for h in range(QH):
                    e = nc.vector.max(top8[:, 0, h], bank_u[:, P * h:P * h + P])
                e.then_inc(topk_step, 1)
                dve.wait_ge(topk_step, base + 1)
                nc.vector.tensor_scalar(neg_max[:, u % 4].unsqueeze(2), top8[:, 0, :, 0:1], -1.0, None,
                                        ALU.mult)
                for h in range(QH):
                    e = nc.vector.match_replace(l[:, h], top8[:, 0, h], bank_u[:, P * h:P * h + P], GONE)
                e.then_inc(topk_step, 1)
                dve.wait_ge(topk_step, base + 2)
                dve.sem_inc(scored, 1)
                for h in range(QH):
                    e = nc.vector.max(top8[:, 1, h], l[:, h])
                e.then_inc(topk_step, 1)
                dve.wait_ge(topk_step, base + 3)
                dve.sem_inc(dve_passed, 1)
                for h in range(QH):
                    e = nc.vector.match_replace(l[:, h], top8[:, 1, h], l[:, h], GONE)
                    if h == 0:
                        e.then_inc(topk_step, 1)
                e.then_inc(left_ready, 1)

            with dve.Fori(0, ITERS) as i:
                nc.vector.tensor_copy(mod_now[:].rearrange("p s j -> p (s j)"),
                                      mod_all[:].rearrange("p (i s) j -> p i (s j)", s=SLOTS)[:, i]).then_inc(mod_ready, 1)
                for t in STEPS:
                    if 0 <= t < UNITS:
                        dve.wait_ge(scores_ready, i * UNITS + t + 1)
                        dve.sem_inc(dve_passed, 1)
                        if t // (4 * SLOTS) == CROSS:
                            top_k(i, t)
                        else:
                            nc.vector.tensor_reduce(neg_max[:, t % 4], score_bank[t % 3][:].rearrange("p (h t) -> p h t", t=P),
                                                    AX.X, ALU.max, negate=True).then_inc(scored, 1)
                    u = t - 3
                    if 0 <= u < UNITS and u % 4 == 3:
                        ph = u // 4
                        dve.wait_ge(o_ready, i * PHASES + ph + 1)
                        nc.vector.reciprocal(inv_sum[:], o_view[:, :, 1]).then_inc(inv_done, 1)
                        dve.wait_ge(inv_done, i * PHASES + ph + 1)
                        nc.vector.tensor_tensor(o_t[:], o_view[:, :, 0], inv_sum[:], ALU.mult).then_inc(o_t_ready, 1)
                    for part in PLAN.get(t, ()):
                        name, kind, s = part
                        n, m = DENSE[part], NTH[part]
                        d = dense_bank[n % 2]
                        if name == "stats":
                            src = {SELF: x_in, CTX: ctx_in}.get(kind, x_mid)[:, s, :]
                            if kind == SELF:
                                dve.wait_ge(x_loaded[s], (i + 1) * 16)
                            elif kind == CTX:
                                dve.wait_ge(ctx_loaded[s], (i + 1) * 16)
                            else:
                                before = {CROSS: SELF, MLP: CROSS, LAST: MLP}[kind]
                                dve.wait_ge(x_done, i * N_OUT + NTH["out", before, s] + 1)
                            nc.vector.bn_stats(ln_stats[:, m % 4], src).then_inc(bn_done, 1)
                            dve.wait_ge(bn_done, i * COUNT["stats"] + m + 1)
                            dve.sem_inc(dve_passed, 1)
                            nc.vector.bn_aggr(ln_mv[:, m % 4], ln_stats[:, m % 4]).then_inc(stats_done, 1)
                        if name == "norm":
                            src = {SELF: x_in, CTX: ctx_in}.get(kind, x_mid)[:, s, :]
                            dve.wait_ge(rstd_done, i * COUNT["stats"] + NTH["stats", kind, s] + 1)
                            g = NTH["stats", kind, s] % 4
                            nc.vector.tensor_scalar(x_norm[:, m % 3], src, ln_mv[:, g, 0:1], ln_rstd[:, g, 0:1],
                                                    ALU.subtract, ALU.mult).then_inc(norm_done, 1)
                        if name == "q":
                            r = phase_of(kind, s) % RING
                            b = bias_cols[:, QUERY_BIAS[kind]:QUERY_BIAS[kind] + CK]
                            dve.wait_ge(dense_ready, i * N_DENSE + n + 1)
                            nc.vector.tensor_tensor(q_t[:, r], d[:, 0:C].rearrange("p (c t) -> p c t", t=P),
                                                    b.unsqueeze(2).broadcast_to([P, CK, P]), ALU.add).then_inc(q_ready, 1)
                            dve.wait_ge(q_ready, i * COUNT["q"] + m + 1)
                            dve.sem_inc(dense_free[n % 2], 1)
                        if name == "kv":
                            r = phase_of(kind, s) % RING
                            b = bias_cols[:, KEY_BIAS[kind]:KEY_BIAS[kind] + CK]
                            dve.wait_ge(dense_ready, i * N_DENSE + n + 1)
                            nc.vector.tensor_tensor(k_t[:, m % 3], d[:, 0:C].rearrange("p (c t) -> p c t", t=P),
                                                    b.unsqueeze(2).broadcast_to([P, CK, P]), ALU.add).then_inc(k_ready, 1)
                            v = v_pad[:, r].rearrange("p g a j -> p (g a j)").rearrange("p (g w) -> p g w", w=64)
                            for odd in range(2):
                                src = d[:, C:2 * C].rearrange("p (g a j) -> p g a j", a=2, j=D)[:, :, odd]
                                bv = b_value[:, kind].rearrange("p (g a j) -> p g a j", a=2, j=D)[:, :, odd]
                                e = nc.vector.tensor_tensor(v[:, :, 48 * odd:48 * odd + D], src, bv, ALU.add)
                            e.then_inc(v_ready, 1)
                            dve.wait_ge(v_ready, i * COUNT["kv"] + m + 1)
                            dve.sem_inc(dense_free[n % 2], 1)
                        if name == "out":
                            dve.wait_ge(dense_ready, i * N_DENSE + n + 1)
                            skip = i * COUNT["skip"] + NTH["skip", kind, s] + 1
                            if kind == LAST:
                                dve.wait_ge(skip_ready, skip)
                                nc.vector.tensor_tensor(x_mid[:, s, :], d[:, 0:C], x_skip[:, s, :],
                                                        ALU.add).then_inc(x_done, 1)
                                dve.wait_ge(x_done, i * N_OUT + m + 1)
                                dve.sem_inc(dense_free[n % 2], 1)
                            else:
                                g = gates[:, s, GATE[kind] * C:(GATE[kind] + 1) * C]
                                dve.wait_ge(gates_loaded[s], (i + 1) * 16)
                                nc.vector.tensor_tensor(gated[:], d[:, 0:C], g, ALU.mult).then_inc(dense_free[n % 2], 1)
                                dve.wait_ge(dense_free[n % 2], i * (N_DENSE // 2) + n // 2 + 2)
                                dve.wait_ge(skip_ready, skip)
                                nc.vector.tensor_tensor(x_mid[:, s, :], gated[:], x_skip[:, s, :],
                                                        ALU.add).then_inc(x_done, 1)
                        if name == "up":
                            dve.wait_ge(dense_ready, i * N_DENSE + n + 1)
                            b = bias_cols[:, 38 + 4 * kind:42 + 4 * kind]
                            nc.vector.tensor_tensor(half_a[:, m % 2], d[:].rearrange("p (j t) -> p j t", t=P),
                                                    b.unsqueeze(2).broadcast_to([P, 4, P]), ALU.add).then_inc(half_a_done, 1)
                            dve.wait_ge(half_a_done, i * COUNT["up"] + m + 1)
                            dve.sem_inc(dense_free[n % 2], 1)
                        if name == "glu":
                            dve.wait_ge(tanh_done, i * COUNT["glu"] + m + 1)
                            nc.vector.scalar_tensor_tensor(
                                out=tanh_a[:, m % 2].rearrange("p j t -> p (j t)"),
                                in0=tanh_a[:, m % 2].rearrange("p j t -> p (j t)"), scalar=1.0,
                                in1=half_a[:, m % 2].rearrange("p j t -> p (j t)"),
                                op0=ALU.add, op1=ALU.mult).then_inc(silu_done, 1)

        @block.tensor
        def _(pe):
            pe.wait_ge(consts_ready, 1)
            pe.wait_ge(rows_loaded, 9 * 16)
            nc.tensor.transpose(dense_bank[0][:, 0:NBIAS], bias_rows[:], ident[0:NBIAS, 0:NBIAS]).then_inc(setup_pe, 1)
            pe.wait_ge(setup_dve, 2)
            for c in range(CK):
                e = nc.tensor.transpose(dense_bank[1][:, B * c:B * c + B], cond_silu[:, P * c:P * c + P], ident[0:B, 0:B])
            e.then_inc(setup_pe, 1)
            pe.wait_ge(ada_loaded, 3 * 16)
            pe.wait_ge(setup_dve, 5)
            cols = []
            for k in range(3):
                cols += [w_ada[:, :, C * (3 * k + 1) + P * c:C * (3 * k + 1) + P * c + P] for c in range(CK)]
                cols += [w_ada[:, :, C * 3 * k + P * c:C * 3 * k + P * c + P] for c in range(CK)]
            for w in (ss_q, ss_kv):
                cols += [w[:, :, P * c:P * c + P] for c in range(4)]
            for j, w in enumerate(cols):
                for c in range(CK):
                    e = nc.tensor.matmul(score_bank[0][:, B * j:B * j + B], w[:, c], silu_t[:, c],
                                         start=(c == 0), stop=(c == CK - 1))
            e.then_inc(setup_pe, 1)
            for k in range(3):
                dst = score_bank[1][0:B, C * k:C * k + C] if k < 2 else score_bank[2][0:B, 0:C]
                for c in range(CK):
                    e = nc.tensor.matmul(dst, silu_t[:, c], w_ada[:, c, C * (3 * k + 2):C * (3 * k + 3)],
                                         start=(c == 0), stop=(c == CK - 1))
            e.then_inc(setup_pe, 1)
            for w in w_loaded.values():
                pe.wait_ge(w, 16)
            pe.wait_ge(w_scaled, 4)
            pe.wait_ge(consts_ready, 2)
            pe.wait_ge(setup_dve, 8)

            with pe.Fori(0, ITERS) as i:
                for t in STEPS:
                    if 0 <= t < UNITS:
                        ph, c, blk = t // 4, t % 4 // 2, 4 * (t % 2)
                        kind, s, r = ph // SLOTS, ph % SLOTS, ph % RING
                        if t % 4 == 0:
                            pe.wait_ge(q_ready, i * COUNT["q"] + NTH["q", kind, s] + 1)
                            pe.wait_ge(k_placed[r], i * FILLS * 16 * HC + 16 * HC * (ph // RING + 1))
                        nc.tensor.matmul(score_bank[t % 3][:], q_t[:, r, c],
                                         k_blocks[:, r, c, blk:blk + 4].rearrange("p h t -> p (h t)"),
                                         start=True, stop=True).then_inc(scores_ready, 1)
                    u = t - 2
                    if 0 <= u < UNITS:
                        if u // (4 * SLOTS) == CROSS:
                            pe.wait_ge(top_ready, i * 4 * SLOTS + u - 4 * SLOTS + 1)
                            src = left
                        else:
                            pe.wait_ge(probs_ready, i * UNITS + u + 1)
                            src = probs
                        for h in range(QH):
                            e = nc.tensor.transpose(turn_bank[u % 2][:, P * h:P * h + P], src[:, u % 3, h], ident[:])
                        e.then_inc(turned, 1)
                    u = t - 3
                    if 0 <= u < UNITS:
                        ph, c = u // 4, u % 4 // 2
                        kind, s, r = ph // SLOTS, ph % SLOTS, ph % RING
                        if u % 4 == 0:
                            pe.wait_ge(v_ready, i * COUNT["kv"] + NTH["kv", kind, s] + 1)
                            if ph:
                                pe.wait_ge(o_t_ready, i * PHASES + ph)
                        pe.wait_ge(probs_t_ready, i * UNITS + u + 1)
                        for what in range(2):
                            for g in range(2):
                                lane = 32 * (2 * (u % 2) + g)
                                for odd in range(2):
                                    w = v_pad[:, r, 2 * (u % 4) + g, odd] if what == 0 else one_cols[:, odd]
                                    e = nc.tensor.matmul(o_view[lane:lane + 32, c, what], w, probs_t[:, u % 3, 2 * g + odd],
                                                         start=(odd == 0), stop=(odd == 1))
                        if u % 4 == 3:
                            e.then_inc(o_ready, 1)
                    for part in PLAN.get(t, ()):
                        name, kind, s = part
                        n = DENSE[part]
                        d = dense_bank[n % 2]
                        if name in DENSE_USES:
                            pe.wait_ge(dense_free[n % 2], i * (N_DENSE // 2) + n // 2 + 1)
                        if name == "turn":
                            pe.wait_ge(norm_done, i * COUNT["norm"] + NTH["norm", kind, s] + 1)
                            g = NTH["norm", kind, s] % 3
                            for c in range(CK):
                                e = nc.tensor.transpose(d[:, P * c:P * c + P], x_norm[:, g, P * c:P * c + P], ident[:])
                            e.then_inc(dense_ready, 1)
                        if name == "turn_ctx":
                            pe.wait_ge(norm_done, i * COUNT["norm"] + NTH["norm", kind, s] + 1)
                            g = NTH["norm", kind, s] % 3
                            for c in range(CK):
                                nc.tensor.transpose(d[:, P * c:P * c + P], ctx_in[:, s, P * c:P * c + P], ident[:])
                            for c in range(CK):
                                e = nc.tensor.transpose(d[:, P * (2 + c):P * (3 + c)], x_norm[:, g, P * c:P * c + P], ident[:])
                            e.then_inc(dense_ready, 1)
                        if name == "q":
                            pe.wait_ge(h_ready, (i * COUNT["turn"] + NTH["turn", kind, s] + 1) * 2)
                            for j in range(CK):
                                for c in range(CK):
                                    e = nc.tensor.matmul(d[:, P * j:P * j + P], w_query[kind][:, c, P * j:P * j + P],
                                                         h_t[:, s, c], start=(c == 0), stop=(c == CK - 1))
                            e.then_inc(dense_ready, 1)
                        if name == "kv":
                            src = {SELF: h_t[:, s], CROSS: ctx_t[:, 0], LAST: ctx_norm_t[:, s % 3]}[kind]
                            turn = ("turn", SELF, s) if kind == SELF else ("turn_ctx", CTX, s)
                            pe.wait_ge(h_ready, (i * COUNT["turn"] + NTH[turn] + 1) * 2)
                            for j in range(CK):
                                for c in range(CK):
                                    nc.tensor.matmul(d[:, P * j:P * j + P], w_key[kind][:, c, P * j:P * j + P],
                                                     src[:, c], start=(c == 0), stop=(c == CK - 1))
                            for c in range(CK):
                                e = nc.tensor.matmul(d[:, C:2 * C], src[:, c], w_value[kind][:, c],
                                                     start=(c == 0), stop=(c == CK - 1))
                            e.then_inc(dense_ready, 1)
                        if name == "out" and kind != MLP:
                            pe.wait_ge(o_t_ready, i * PHASES + phase_of(kind, s) + 1)
                            for c in range(CK):
                                e = nc.tensor.matmul(d[:, 0:C], o_t[:, c], w_out[kind][:, c],
                                                     start=(c == 0), stop=(c == CK - 1))
                            e.then_inc(dense_ready, 1)
                        if name == "up":
                            if kind == 0:
                                pe.wait_ge(h_ready, (i * COUNT["turn"] + NTH["turn", MLP, s] + 1) * 2)
                            for half in range(2):
                                d = dense_bank[(n + half) % 2]
                                if half:
                                    pe.wait_ge(dense_free[(n + 1) % 2], i * (N_DENSE // 2) + (n + 1) // 2 + 1)
                                for j in range(4):
                                    at = HID * half + P * (4 * kind + j)
                                    for c in range(CK):
                                        e = nc.tensor.matmul(d[:, P * j:P * j + P], w_m1[:, c, at:at + P], h_t[:, s, c],
                                                             start=(c == 0), stop=(c == CK - 1))
                                e.then_inc(dense_ready, 1)
                        if name == "out" and kind == MLP:
                            pe.wait_ge(glu_done, i * COUNT["glu"] + NTH["glu", 1, s] + 1)
                            for j in range(HB):
                                e = nc.tensor.matmul(d[:, 0:C], glu[:, j], w_m2[:, j],
                                                     start=(j == 0), stop=(j == HB - 1))
                            e.then_inc(dense_ready, 1)


PLAN_SKIPS_LAST = [NTH["skip", LAST, s] for s in range(SLOTS)]

_INS = ["x", "cond_1024", "ctx_1024", "L0_xcond_w_ada", "L0_xcond_b_ada", "L0_xcond_w_qkv", "L0_xcond_b_qkv",
        "L0_xcond_w_so", "L0_xcond_b_so", "L0_xcond_w_q", "L0_xcond_b_q", "L0_xcond_w_kv", "L0_xcond_b_kv",
        "L0_xcond_w_co", "L0_xcond_b_co", "L0_xcond_w_m1", "L0_xcond_b_m1", "L0_xcond_w_m2", "L0_xcond_b_m2",
        "L1_xcond_Wq", "L1_xcond_bq", "L1_xcond_Wkv", "L1_xcond_bkv", "L1_xcond_Wp", "L1_xcond_bp",
        "L1_xcond_Wss_q", "L1_xcond_bss_q", "L1_xcond_Wss_kv", "L1_xcond_bss_kv"]


def kernel(**inputs):
    import numpy as np
    import concourse.bacc as bacc
    from concourse import mybir as _mybir
    from concourse.bass_utils import run_bass_kernel_spmd

    nc = bacc.Bacc("TRN2", target_bir_lowering=False, num_devices=1)
    arrays, aps = {}, {}
    for name in _INS:
        arr = np.ascontiguousarray(inputs[name])
        arrays[f"in_{name}"] = arr
        aps[name] = nc.dram_tensor(f"in_{name}", arr.shape, _mybir.dt.from_np(arr.dtype), kind="ExternalInput").ap()
    out = nc.dram_tensor("out_y", (B, P, C), F32, kind="ExternalOutput").ap()
    block_kernel(nc, aps, out)
    r = run_bass_kernel_spmd(nc, [arrays], core_ids=[0])
    return r.results[0]["out_y"]
```

```python
from contextlib import ExitStack

import concourse.bass as bass
from concourse import mybir

F32 = mybir.dt.float32
ALU = mybir.AluOpType
ACT = mybir.ActivationFunctionType
AX = mybir.AxisListType

P = 128
B = 16
C = 256
CK = C // P
H = 16
D = C // H
HC = P // D
HID = 1024
HB = HID // P
SLOTS = 4
ITERS = B // SLOTS
QH = 4
PHASES = 3 * SLOTS
UNITS = PHASES * (H // QH)
RING = 6
FILLS = PHASES // RING
GONE = -(2.0 ** 127)

SELF, CROSS, LAST, MLP, CTX = range(5)
LNS = {SELF: 1e-6, CROSS: 1e-6, MLP: 1e-6, LAST: 1e-5, CTX: 1e-5}
NMOD = 4 * len(LNS)
NBIAS = 18 + 4 + 4 + 4 + 2 + 2 + 2 + 2 + 16

SCORE_AHEAD, TURN_LAG, SUM_LAG, O_LAG = 1, 3, 4, 5
EARLY = ("norm", "glu")

PLAN, AHEAD = {}, {}


def _put(step, *part):
    if step < 0:
        AHEAD.setdefault(step + UNITS, []).append(part)
    else:
        PLAN.setdefault(step, []).append(part)


for _s in range(SLOTS):
    _first = 4 * _s
    for _step, *_part in (
            (-8, "stats", SELF), (-6, "norm", SELF), (-6, "turn", SELF), (-5, "kv", SELF), (-5, "q", SELF),
            (5, "skip", SELF), (8, "out", SELF), (8, "stats", CROSS), (9, "skip", CROSS), (10, "norm", CROSS),
            (10, "turn", CROSS), (12, "q", CROSS), (5, "stats", CTX),
            (7, "norm", CTX), (7, "turn_ctx", CTX), (9, "kv", CROSS), (18, "kv", LAST)):
        _put(_first + _step, *_part, _s)
    _first += 4 * SLOTS
    for _step, *_part in (
            (8, "out", CROSS), (8, "stats", MLP), (9, "norm", MLP), (9, "turn", MLP), (9, "skip", MLP),
            (10, "up", 0), (11, "glu", 0), (11, "up", 1), (12, "glu", 1), (12, "out", MLP),
            (12, "stats", LAST), (13, "norm", LAST), (13, "turn", LAST), (13, "skip", LAST),
            (14, "q", LAST), (24, "out", LAST)):
        _put(_first + _step, *_part, _s)
STEPS = range(-SCORE_AHEAD, max(max(PLAN), UNITS + O_LAG - 1) + 1)

DENSE_USES = {"q": 1, "kv": 1, "turn": 1, "turn_ctx": 1, "out": 1, "up": 2}
NTH, COUNT = {}, {}
for _plan in (AHEAD, PLAN):
    for _t in sorted(_plan):
        for _part in _plan[_t]:
            _sort = {"turn_ctx": "turn"}.get(_part[0], _part[0])
            NTH[_part] = COUNT.get(_sort, 0)
            COUNT[_sort] = NTH[_part] + 1
for _t in sorted(AHEAD):
    for _part in AHEAD[_t]:
        for _u in PLAN:
            for _other in PLAN[_u]:
                assert _u <= _t or _other[0].split("_")[0] != _part[0].split("_")[0], (_part, _other)
DENSE, DENSE_FIRST, N_DENSE, N_FIRST = {}, {}, 0, 0
for _t in STEPS:
    for _part in PLAN.get(_t, []) + AHEAD.get(_t, []):
        DENSE[_part] = N_DENSE
        N_DENSE += DENSE_USES.get(_part[0], 0)
for _t in sorted(AHEAD):
    for _part in AHEAD[_t]:
        DENSE_FIRST[_part] = N_FIRST
        N_FIRST += DENSE_USES.get(_part[0], 0)
assert N_DENSE % 2 == 0 and N_FIRST % 2 == 0
DENSE_LAST, _n = {}, 0
for _t in STEPS:
    for _part in PLAN.get(_t, []):
        DENSE_LAST[_part] = _n
        _n += DENSE_USES.get(_part[0], 0)
GATE = {SELF: 0, CROSS: 1, MLP: 2}
N_OUT = COUNT["out"]
KV_ORDER = [part[1:] for part in sorted((q for q in NTH if q[0] == "kv"), key=NTH.get)]
QUERY_BIAS = {SELF: 26, CROSS: 30, LAST: 34}
KEY_BIAS = {SELF: 28, CROSS: 32, LAST: 36}


def block_kernel(nc, a, out):
    with ExitStack() as ctx:
        def sb(name, *shape):
            return ctx.enter_context(nc.sbuf_tensor(name, list(shape), F32))

        def bank(name):
            return ctx.enter_context(nc.psum_tensor(name, [P, 512], F32))

        def sem(name):
            return ctx.enter_context(nc.semaphore(name))

        w_qkv = sb("w_qkv", P, CK, 3 * C)
        w_so = sb("w_so", P, CK, C)
        w_q = sb("w_q", P, CK, C)
        w_kv = sb("w_kv", P, CK, 2 * C)
        w_co = sb("w_co", P, CK, C)
        w_m1 = sb("w_m1", P, CK, 2 * HID)
        w_m2 = sb("w_m2", P, HB, C)
        l_q = sb("l_q", P, CK, C)
        l_kv = sb("l_kv", P, CK, 2 * C)
        l_p = sb("l_p", P, CK, C)
        w_query = {SELF: w_qkv[:, :, 0:C], CROSS: w_q[:], LAST: l_q[:]}
        w_key = {SELF: w_qkv[:, :, C:2 * C], CROSS: w_kv[:, :, 0:C], LAST: l_kv[:, :, 0:C]}
        w_value = {SELF: w_qkv[:, :, 2 * C:3 * C], CROSS: w_kv[:, :, C:2 * C], LAST: l_kv[:, :, C:2 * C]}
        w_out = {SELF: w_so, CROSS: w_co, LAST: l_p}
        b_value = sb("b_value", P, 3, C)
        b_out = sb("b_out", P, 4, C)
        bias_rows = sb("bias_rows", NBIAS, P)
        bias_cols = sb("bias_cols", P, NBIAS)
        mod_bias = sb("mod_bias", P, NMOD)
        silu_t = sb("silu_t", P, CK, B)
        mod_all = sb("mod_all", P, B, NMOD)
        mod_now = sb("mod_now", P, SLOTS, NMOD)
        ident = sb("ident", P, P)
        minus_half = sb("minus_half", P, 1)
        one_cols = sb("one_cols", P, 2, 32)
        x_in = sb("x_in", P, SLOTS, C)
        ctx_in = sb("ctx_in", P, SLOTS, C)
        gates = sb("gates", P, SLOTS, 3 * C)
        x_mid = sb("x_mid", P, SLOTS, C)
        x_skip = sb("x_skip", P, SLOTS, C)
        gated = sb("gated", P, C)
        x_norm = sb("x_norm", P, 3, C)
        ln_stats = sb("ln_stats", P, 4, 6)
        ln_mv = sb("ln_mv", P, 4, 2)
        ln_var = sb("ln_var", P, 4, 1)
        ln_rstd = sb("ln_rstd", P, 4, 1)
        h_t = sb("h_t", P, SLOTS, CK, P)
        ctx_t = sb("ctx_t", P, 1, CK, P)
        ctx_norm_t = sb("ctx_norm_t", P, 3, CK, P)
        q_t = sb("q_t", P, RING, CK, P)
        k_t = sb("k_t", P, 3, CK, P)
        k_blocks = sb("k_blocks", P, RING, CK, HC, P)
        v_pad = sb("v_pad", P, RING, H // 2, 2, 32)
        neg_max = sb("neg_max", P, 4, QH)
        probs = sb("probs", P, 4, QH, P)
        left = sb("left", P, 4, QH, P)
        top8 = sb("top8", P, 2, QH, 8)
        probs_t = sb("probs_t", P, 3, QH, P)
        inv_sum = sb("inv_sum", P, CK, P)
        o_t = sb("o_t", P, CK, P)
        half_a = sb("half_a", P, 2, 4, P)
        tanh_a = sb("tanh_a", P, 2, 4, P)
        lin_b = sb("lin_b", P, 2, 4, P)
        glu = sb("glu", P, HB, P)
        gate_rows = glu[0:B].rearrange("p j t -> p (j t)")[:, 0:3 * C]
        gates_dram = nc.dram_tensor("gates_dram", (B, 3 * C), F32).ap()
        arena = k_blocks[:].rearrange("p r c h t -> p (r c h t)")
        NADA = 9 * C
        w_ada = arena[:, 0:CK * NADA].rearrange("p (c n) -> p c n", c=CK)
        ss_q = arena[:, CK * NADA:CK * (NADA + 2 * C)].rearrange("p (c n) -> p c n", c=CK)
        ss_kv = arena[:, CK * (NADA + 2 * C):CK * (NADA + 4 * C)].rearrange("p (c n) -> p c n", c=CK)

        spare = arena[0:B, CK * (NADA + 4 * C):]
        gate_bias = spare[:, 0:3 * C]
        cond, cond_tanh, cond_silu = (spare[:, n * C:(n + 1) * C] for n in (3, 4, 5))

        score_bank = [bank(f"score_bank{n}") for n in range(3)]
        turn_bank = [bank(f"turn_bank{n}") for n in range(2)]
        o_bank = bank("o_bank")
        dense_bank = [bank(f"dense_bank{n}") for n in range(2)]
        o_view = o_bank[:].rearrange("p (c k t) -> p c k t", c=CK, k=2)

        cond_loaded = sem("cond_loaded")
        ada_loaded = sem("ada_loaded")
        rows_loaded = sem("rows_loaded")
        bcast_loaded = sem("bcast_loaded")
        gate_bias_loaded = sem("gate_bias_loaded")
        w_loaded = {k: sem(f"w_loaded_{k}") for k in ("qkv", "so", "q", "kv", "co", "m1", "m2", "lq", "lkv", "lp")}
        x_loaded = [sem(f"x_loaded{s}") for s in range(SLOTS)]
        ctx_loaded = [sem(f"ctx_loaded{s}") for s in range(SLOTS)]
        gates_loaded = [sem(f"gates_loaded{s}") for s in range(SLOTS)]
        gates_stored = sem("gates_stored")
        k_placed = [sem(f"k_placed{r}") for r in range(RING)]
        y_stored = sem("y_stored")
        y_gone = sem("y_gone")
        ident_step = sem("ident_step")
        consts_ready = sem("consts_ready")
        blocks_zeroed = sem("blocks_zeroed")
        w_scaled = sem("w_scaled")
        setup_act = sem("setup_act")
        setup_dve = sem("setup_dve")
        setup_pe = sem("setup_pe")
        dve_passed = sem("dve_passed")
        pool_passed = sem("pool_passed")
        sp_passed = sem("sp_passed")
        mod_ready = sem("mod_ready")
        bn_done = sem("bn_done")
        stats_done = sem("stats_done")
        var_done = sem("var_done")
        rstd_done = sem("rstd_done")
        norm_done = sem("norm_done")
        h_ready = sem("h_ready")
        q_ready = sem("q_ready")
        k_ready = sem("k_ready")
        v_ready = sem("v_ready")
        skip_part = sem("skip_part")
        skip_ready = sem("skip_ready")
        gated_done = sem("gated_done")
        x_done = sem("x_done")
        half_a_done = sem("half_a_done")
        tanh_done = sem("tanh_done")
        lin_b_done = sem("lin_b_done")
        silu_done = sem("silu_done")
        glu_done = sem("glu_done")
        dense_ready = sem("dense_ready")
        dense_free = [sem(f"dense_free{n}") for n in range(2)]
        scores_ready = sem("scores_ready")
        topk_step = sem("topk_step")
        scored = sem("scored")
        left_ready = sem("left_ready")
        probs_ready = sem("probs_ready")
        mask_done = sem("mask_done")
        top_ready = sem("top_ready")
        turned = sem("turned")
        probs_t_ready = sem("probs_t_ready")
        o_ready = sem("o_ready")
        inv_done = sem("inv_done")
        o_t_ready = sem("o_t_ready")

        block = ctx.enter_context(nc.Block())

        def phase_of(kind, s):
            return SLOTS * kind + s

        @block.sync
        def _(sp):
            def chunks(w):
                return w.rearrange("(c p) n -> p c n", p=P)

            def rows(v):
                return v.rearrange("(c p) -> c p", p=P)

            sp.dma_start(cond, a["cond_1024"]).then_inc(cond_loaded, 16)
            at = 0
            for v in (a["L0_xcond_b_ada"], a["L1_xcond_bss_q"], a["L1_xcond_bss_kv"],
                      a["L0_xcond_b_qkv"][0:2 * C], a["L0_xcond_b_q"], a["L0_xcond_b_kv"][0:C],
                      a["L1_xcond_bq"], a["L1_xcond_bkv"][0:C], a["L0_xcond_b_m1"]):
                n = v.shape[0] // P
                sp.dma_start(bias_rows[at:at + n, :], rows(v)).then_inc(rows_loaded, 16)
                at += n
            sp.dma_start(w_ada, chunks(a["L0_xcond_w_ada"])).then_inc(ada_loaded, 16)
            sp.dma_start(ss_q, chunks(a["L1_xcond_Wss_q"])).then_inc(ada_loaded, 16)
            sp.dma_start(ss_kv, chunks(a["L1_xcond_Wss_kv"])).then_inc(ada_loaded, 16)
            gate_chunks = a["L0_xcond_b_ada"].rearrange("(k n) -> k n", n=C)[2::3]
            sp.dma_start(gate_bias.rearrange("b (k n) -> b k n", n=C),
                         gate_chunks.partition_broadcast(B)).then_inc(gate_bias_loaded, 16)
            for s in range(SLOTS):
                sp.dma_start(x_in[:, s, :], a["x"][s]).then_inc(x_loaded[s], 16)
                sp.dma_start(ctx_in[:, s, :], a["ctx_1024"][s]).then_inc(ctx_loaded[s], 16)
            for key, dst, src in (("qkv", w_qkv, "L0_xcond_w_qkv"), ("q", w_q, "L0_xcond_w_q")):
                sp.dma_start(dst[:], chunks(a[src])).then_inc(w_loaded[key], 16)
            for n, v in enumerate((a["L0_xcond_b_qkv"][2 * C:3 * C], a["L0_xcond_b_kv"][C:2 * C],
                                   a["L1_xcond_bkv"][C:2 * C])):
                sp.dma_start(b_value[:, n, :], v.partition_broadcast(P)).then_inc(bcast_loaded, 16)
            for n, v in enumerate((a["L0_xcond_b_so"], a["L0_xcond_b_co"], a["L1_xcond_bp"],
                                   a["L0_xcond_b_m2"])):
                sp.dma_start(b_out[:, n, :], v.partition_broadcast(P)).then_inc(bcast_loaded, 16)
            for key, dst, src in (("so", w_so, "L0_xcond_w_so"), ("kv", w_kv, "L0_xcond_w_kv"),
                                  ("co", w_co, "L0_xcond_w_co"), ("lq", l_q, "L1_xcond_Wq"),
                                  ("lkv", l_kv, "L1_xcond_Wkv"), ("m1", w_m1, "L0_xcond_w_m1"),
                                  ("m2", w_m2, "L0_xcond_w_m2"), ("lp", l_p, "L1_xcond_Wp")):
                sp.dma_start(dst[:], chunks(a[src])).then_inc(w_loaded[key], 16)
            sp.wait_ge(setup_dve, 8)
            sp.dma_start(gates_dram, gate_rows).then_inc(gates_stored, 16)
            sp.wait_ge(gates_stored, 16)
            for s in range(SLOTS):
                sp.dma_start(gates[:, s, :], gates_dram[s].partition_broadcast(P)).then_inc(gates_loaded[s], 16)
            sp.sem_inc(y_gone, 1)
            sp.wait_ge(blocks_zeroed, 1)

            def place_k(part, i):
                r = phase_of(*part[1:]) % RING
                sp.wait_ge(k_ready, i * COUNT["kv"] + NTH[part] + 1)
                for h in range(HC):
                    rows_h = slice(D * h, D * h + D)
                    sp.dma_start(k_blocks[rows_h, r, :, h, :], k_t[rows_h, NTH[part] % 3]).then_inc(k_placed[r], 16)

            def body(i, more):
                for t in STEPS:
                    for part in PLAN.get(t, ()):
                        name, kind, s = part
                        nxt = (i + 1) * SLOTS + s
                        if name == "kv":
                            place_k(part, i)
                            if kind == CROSS and more:
                                sp.dma_start(ctx_in[:, s, :], a["ctx_1024"][nxt]).then_inc(ctx_loaded[s], 16)
                        if name == "out":
                            if kind == LAST or more:
                                sp.wait_ge(x_done, i * N_OUT + NTH[part] + 1)
                                sp.sem_inc(sp_passed, 1)
                            if kind == LAST:
                                sp.dma_start(out[i * SLOTS + s], x_mid[:, s, :]).then_inc(y_stored, 16)
                            if kind == SELF and more:
                                sp.dma_start(x_in[:, s, :], a["x"][nxt]).then_inc(x_loaded[s], 16)
                            if kind == MLP and more:
                                sp.dma_start(gates[:, s, :], gates_dram[nxt].partition_broadcast(P)).then_inc(gates_loaded[s], 16)
                    for part in AHEAD.get(t, ()) if more else ():
                        if part[0] == "kv":
                            place_k(part, i + 1)
                sp.wait_ge(y_stored, (i + 1) * 16 * SLOTS)
                sp.sem_inc(y_gone, 1)

            for t in sorted(AHEAD):
                for part in AHEAD[t]:
                    if part[0] == "kv":
                        place_k(part, 0)
            with sp.Fori(0, ITERS - 1) as i:
                body(i, True)
            body(ITERS - 1, False)

        @block.gpsimd
        def _(pool):
            nc.gpsimd.memset(ident[:], 0.0).then_inc(ident_step, 1)
            pool.wait_ge(ident_step, 1)
            nc.gpsimd.affine_select(out=ident[:], in_=ident[:], compare_op=ALU.not_equal, fill=1.0,
                                    base=0, pattern=[[-1, P]], channel_multiplier=1).then_inc(consts_ready, 1)
            nc.gpsimd.memset(minus_half[:], -0.5)
            nc.gpsimd.memset(v_pad[:], 0.0)
            nc.gpsimd.memset(one_cols[:], 0.0).then_inc(ident_step, 1)
            pool.wait_ge(ident_step, 2)
            nc.gpsimd.memset(one_cols[:, 0, 0:D], 1.0)
            nc.gpsimd.memset(one_cols[:, 1, D:2 * D], 1.0).then_inc(consts_ready, 1)
            for key, w in (("qkv", w_query[SELF]), ("q", w_query[CROSS]), ("lq", w_query[LAST])):
                pool.wait_ge(w_loaded[key], 16)
                nc.gpsimd.tensor_scalar(w, w, 0.25, 1.0, ALU.mult, ALU.mult).then_inc(w_scaled, 1)
            pool.wait_ge(w_loaded["m1"], 16)
            nc.gpsimd.tensor_scalar(w_m1[:, :, 0:HID], w_m1[:, :, 0:HID], 0.5, 1.0, ALU.mult,
                                    ALU.mult).then_inc(w_scaled, 1)
            pool.wait_ge(bcast_loaded, 7 * 16)
            pool.wait_ge(consts_ready, 2)

            def dense_part(part, i, base, half, n_dense):
                name, kind, s = part
                n = NTH[part]
                if name == "stats":
                    pool.wait_ge(stats_done, i * COUNT["stats"] + n + 1)
                    pool.sem_inc(pool_passed, 1)
                    nc.gpsimd.tensor_scalar(ln_var[:, n % 4], ln_mv[:, n % 4, 1:2], LNS[kind], 1.0,
                                            ALU.add, ALU.mult).then_inc(var_done, 1)
                    pool.wait_ge(var_done, i * COUNT["stats"] + n + 1)
                    nc.gpsimd.tensor_tensor(ln_rstd[:, n % 4], ln_var[:, n % 4], minus_half[:],
                                            ALU.pow).then_inc(rstd_done, 1)
                if name == "skip":
                    x_old = x_in if kind == SELF else x_mid
                    if kind == SELF:
                        pool.wait_ge(x_loaded[s], (i + 1) * 16)
                        pool.wait_ge(gates_loaded[s], (i + 1) * 16)
                    else:
                        before = {CROSS: SELF, MLP: CROSS, LAST: MLP}[kind]
                        pool.wait_ge(x_done, i * N_OUT + NTH["out", before, s] + 1)
                    bias = b_out[:, {SELF: 0, CROSS: 1, LAST: 2, MLP: 3}[kind], :]
                    if kind in GATE:
                        g = gates[:, s, GATE[kind] * C:(GATE[kind] + 1) * C]
                        nc.gpsimd.tensor_tensor(x_skip[:, s, :], bias, g, ALU.mult).then_inc(skip_part, 1)
                        m = n - sum(1 for q in PLAN_SKIPS_LAST if q < n)
                        pool.wait_ge(skip_part, i * (COUNT["skip"] - SLOTS) + m + 1)
                        bias = x_skip[:, s, :]
                    nc.gpsimd.tensor_tensor(x_skip[:, s, :], x_old[:, s, :], bias,
                                            ALU.add).then_inc(skip_ready, 1)
                if name == "glu":
                    pool.wait_ge(silu_done, i * COUNT["glu"] + n + 1)
                    pool.wait_ge(lin_b_done, i * COUNT["glu"] + n + 1)
                    nc.gpsimd.tensor_tensor(glu[:, 4 * kind:4 * kind + 4], tanh_a[:, n % 2],
                                            lin_b[:, n % 2], ALU.mult).then_inc(glu_done, 1)

            def dense_parts(i, t, more, early):
                for part in PLAN.get(t, ()):
                    if (part[0] in ("stats", "glu")) == early:
                        dense_part(part, i, N_FIRST + i * N_DENSE, N_FIRST // 2 + i * (N_DENSE // 2),
                                   (DENSE if more else DENSE_LAST)[part])
                for part in AHEAD.get(t, ()) if more else ():
                    if (part[0] in ("stats", "glu")) == early:
                        dense_part(part, i + 1, N_FIRST + i * N_DENSE, N_FIRST // 2 + i * (N_DENSE // 2), DENSE[part])

            def body(i, more):
                for t in STEPS:
                    dense_parts(i, t, more, True)
                    if 0 <= t < UNITS and SLOTS * 4 <= t < 2 * SLOTS * 4:
                        n = t - SLOTS * 4
                        pool.wait_ge(left_ready, i * 4 * SLOTS + n + 1)
                        pool.sem_inc(pool_passed, 1)
                        nc.gpsimd.tensor_scalar(left[:, t % 4], left[:, t % 4], GONE, None,
                                                ALU.is_equal).then_inc(mask_done, 1)
                        pool.wait_ge(mask_done, i * 4 * SLOTS + n + 1)
                        pool.wait_ge(probs_ready, i * UNITS + t + 1)
                        nc.gpsimd.tensor_tensor(left[:, t % 4], left[:, t % 4], probs[:, t % 4],
                                                ALU.mult).then_inc(top_ready, 1)
                    dense_parts(i, t, more, False)

            for t in sorted(AHEAD):
                for part in AHEAD[t]:
                    dense_part(part, 0, 0, 0, DENSE_FIRST[part])
            with pool.Fori(0, ITERS - 1) as i:
                body(i, True)
            body(ITERS - 1, False)


        @block.scalar
        def _(act):
            act.wait_ge(cond_loaded, 16)
            nc.scalar.activation(cond_tanh, cond, ACT.Tanh, scale=0.5).then_inc(setup_act, 1)
            act.wait_ge(setup_dve, 7)
            def dense_part(part, i, base, half, n_dense):
                name, kind, s = part
                n = n_dense
                if name in ("turn", "turn_ctx"):
                    if (name, kind) == ("turn", SELF):
                        act.wait_ge(mod_ready, i * SLOTS + s + 1)
                    act.wait_ge(dense_ready, base + n + 1)
                    d = dense_bank[n % 2]
                    dst, at = (h_t[:, s], 0) if name == "turn" else (ctx_norm_t[:, s % 3], 2 * P)
                    if name == "turn_ctx":
                        nc.scalar.copy(ctx_t[:, 0].rearrange("p c t -> p (c t)"), d[:, 0:2 * P])
                    ln = {SELF: 0, CROSS: 1, MLP: 2, LAST: 3, CTX: 4}[kind]
                    for c in range(CK):
                        e = nc.scalar.activation(dst[:, c], d[:, at + P * c:at + P * c + P], ACT.Identity,
                                                 scale=mod_now[:, s, 4 * ln + c:4 * ln + c + 1],
                                                 bias=mod_now[:, s, 4 * ln + 2 + c:4 * ln + 3 + c])
                        if c == 0:
                            e.then_inc(h_ready, 1)
                    e.then_inc(h_ready, 1)
                    act.wait_ge(h_ready, i * 2 * COUNT["turn"] + 2 * NTH[part] + 2)
                    act.sem_inc(dense_free[n % 2], 1)
                if name == "up":
                    m = NTH[part]
                    act.wait_ge(half_a_done, i * COUNT["up"] + m + 1)
                    nc.scalar.activation(tanh_a[:, m % 2], half_a[:, m % 2], ACT.Tanh).then_inc(tanh_done, 1)
                    act.wait_ge(dense_ready, base + n + 2)
                    for j in range(4):
                        col = 46 + 4 * kind + j
                        e = nc.scalar.activation(lin_b[:, m % 2, j], dense_bank[(n + 1) % 2][:, P * j:P * j + P],
                                                 ACT.Identity, bias=bias_cols[:, col:col + 1])
                    e.then_inc(lin_b_done, 1)
                    act.wait_ge(lin_b_done, i * COUNT["up"] + m + 1)
                    act.sem_inc(dense_free[(n + 1) % 2], 1)

            def dense_parts(i, t, more):
                for part in PLAN.get(t, ()):
                    dense_part(part, i, N_FIRST + i * N_DENSE, N_FIRST // 2 + i * (N_DENSE // 2),
                               (DENSE if more else DENSE_LAST)[part])
                for part in AHEAD.get(t, ()) if more else ():
                    dense_part(part, i + 1, N_FIRST + i * N_DENSE, N_FIRST // 2 + i * (N_DENSE // 2), DENSE[part])

            def body(i, more):
                for t in STEPS:
                    if 0 <= t < UNITS:
                        act.wait_ge(scored, i * UNITS + t + 1)
                        for h in range(QH):
                            e = nc.scalar.activation(probs[:, t % 4, h], score_bank[t % 3][:, P * h:P * h + P],
                                                     ACT.Exp, bias=neg_max[:, t % 4, h:h + 1])
                        e.then_inc(probs_ready, 1)
                    u = t - TURN_LAG
                    if 0 <= u < UNITS:
                        act.wait_ge(turned, i * UNITS + u + 1)
                        nc.scalar.copy(probs_t[:, u % 3].rearrange("p h t -> p (h t)"),
                                       turn_bank[u % 2][:]).then_inc(probs_t_ready, 1)
                    dense_parts(i, t, more)

            for t in sorted(AHEAD):
                for part in AHEAD[t]:
                    dense_part(part, 0, 0, 0, DENSE_FIRST[part])
            with act.Fori(0, ITERS - 1) as i:
                body(i, True)
            body(ITERS - 1, False)


        @block.vector
        def _(dve):
            dve.wait_ge(setup_act, 1)
            nc.vector.scalar_tensor_tensor(out=cond_silu, in0=cond_tanh, scalar=1.0, in1=cond,
                                           op0=ALU.add, op1=ALU.mult).then_inc(setup_dve, 1)
            dve.wait_ge(setup_dve, 1)
            nc.vector.tensor_scalar(cond_silu, cond_silu, 0.5, None, ALU.mult).then_inc(setup_dve, 1)
            dve.wait_ge(setup_pe, 1)
            nc.vector.tensor_copy(bias_cols[:], dense_bank[0][:, 0:NBIAS]).then_inc(setup_dve, 1)
            dve.wait_ge(setup_dve, 3)
            ada = bias_cols[:, 0:18].rearrange("p (k m) -> p k m", m=6)
            ss = bias_cols[:, 18:26].rearrange("p (k m) -> p k m", m=4)
            to_ada = mod_bias[:, 0:12].rearrange("p (k m) -> p k m", m=4)
            to_ss = mod_bias[:, 12:20].rearrange("p (k m) -> p k m", m=4)
            nc.vector.tensor_scalar(to_ada[:, :, 0:2], ada[:, :, 2:4], 1.0, None, ALU.add)
            nc.vector.tensor_scalar(to_ss[:, :, 0:2], ss[:, :, 0:2], 1.0, None, ALU.add)
            nc.vector.tensor_copy(to_ada[:, :, 2:4], ada[:, :, 0:2])
            nc.vector.tensor_copy(to_ss[:, :, 2:4], ss[:, :, 2:4])
            for kind in (SELF, CROSS, LAST):
                q = bias_cols[:, QUERY_BIAS[kind]:QUERY_BIAS[kind] + CK]
                nc.vector.tensor_scalar(q, q, 0.25, None, ALU.mult)
            nc.vector.tensor_scalar(bias_cols[:, 38:38 + HB], bias_cols[:, 38:38 + HB], 0.5, None,
                                    ALU.mult).then_inc(setup_dve, 1)
            dve.wait_ge(setup_pe, 2)
            nc.vector.tensor_copy(silu_t[:].rearrange("p c b -> p (c b)"),
                                  dense_bank[1][:, 0:CK * B]).then_inc(setup_dve, 1)
            dve.wait_ge(setup_pe, 3)
            nc.vector.tensor_tensor(mod_all[:].rearrange("p b j -> p j b"),
                                    score_bank[0][:, 0:NMOD * B].rearrange("p (j b) -> p j b", b=B),
                                    mod_bias[:].unsqueeze(2).broadcast_to([P, NMOD, B]),
                                    ALU.add).then_inc(setup_dve, 1)
            dve.wait_ge(gate_bias_loaded, 16)
            dve.wait_ge(setup_pe, 4)
            nc.vector.tensor_tensor(gate_rows[:, 0:2 * C], score_bank[1][0:B, :], gate_bias[:, 0:2 * C],
                                    ALU.add).then_inc(setup_dve, 1)
            nc.vector.tensor_tensor(gate_rows[:, 2 * C:3 * C], score_bank[2][0:B, 0:C], gate_bias[:, 2 * C:3 * C],
                                    ALU.add).then_inc(setup_dve, 1)
            dve.wait_ge(setup_dve, 8)
            nc.vector.memset(k_blocks[:, 0:3], 0.0)
            nc.vector.memset(k_blocks[:, 3:6], 0.0).then_inc(blocks_zeroed, 1)
            dve.wait_ge(bcast_loaded, 7 * 16)
            dve.sem_inc(dense_free[0], 1)
            dve.sem_inc(dense_free[1], 1)

            def top_k(i, u):
                n = u - 4 * SLOTS
                bank_u, l = score_bank[u % 3], left[:, u % 4]
                base = (i * 4 * SLOTS + n) * 4
                for h in range(QH):
                    e = nc.vector.max(top8[:, 0, h], bank_u[:, P * h:P * h + P])
                e.then_inc(topk_step, 1)
                dve.wait_ge(topk_step, base + 1)
                nc.vector.tensor_scalar(neg_max[:, u % 4].unsqueeze(2), top8[:, 0, :, 0:1], -1.0, None,
                                        ALU.mult)
                for h in range(QH):
                    e = nc.vector.match_replace(l[:, h], top8[:, 0, h], bank_u[:, P * h:P * h + P], GONE)
                e.then_inc(topk_step, 1)
                dve.wait_ge(topk_step, base + 2)
                dve.sem_inc(scored, 1)
                for h in range(QH):
                    e = nc.vector.max(top8[:, 1, h], l[:, h])
                e.then_inc(topk_step, 1)
                dve.wait_ge(topk_step, base + 3)
                dve.sem_inc(dve_passed, 1)
                for h in range(QH):
                    e = nc.vector.match_replace(l[:, h], top8[:, 1, h], l[:, h], GONE)
                    if h == 0:
                        e.then_inc(topk_step, 1)
                e.then_inc(left_ready, 1)

            def dense_part(part, i, base, half, n_dense):
                name, kind, s = part
                n, m = n_dense, NTH[part]
                d = dense_bank[n % 2]
                if name == "stats":
                    src = {SELF: x_in, CTX: ctx_in}.get(kind, x_mid)[:, s, :]
                    if kind == SELF:
                        nc.vector.tensor_copy(mod_now[:, s], mod_all[:].rearrange("p (i s) j -> p i s j", s=SLOTS)[:, i, s]
                                              ).then_inc(mod_ready, 1)
                        dve.wait_ge(x_loaded[s], (i + 1) * 16)
                    elif kind == CTX:
                        dve.wait_ge(ctx_loaded[s], (i + 1) * 16)
                    else:
                        before = {CROSS: SELF, MLP: CROSS, LAST: MLP}[kind]
                        dve.wait_ge(x_done, i * N_OUT + NTH["out", before, s] + 1)
                    nc.vector.bn_stats(ln_stats[:, m % 4], src).then_inc(bn_done, 1)
                    dve.wait_ge(bn_done, i * COUNT["stats"] + m + 1)
                    dve.sem_inc(dve_passed, 1)
                    nc.vector.bn_aggr(ln_mv[:, m % 4], ln_stats[:, m % 4]).then_inc(stats_done, 1)
                if name == "norm":
                    src = {SELF: x_in, CTX: ctx_in}.get(kind, x_mid)[:, s, :]
                    dve.wait_ge(rstd_done, i * COUNT["stats"] + NTH["stats", kind, s] + 1)
                    g = NTH["stats", kind, s] % 4
                    nc.vector.tensor_scalar(x_norm[:, m % 3], src, ln_mv[:, g, 0:1], ln_rstd[:, g, 0:1],
                                            ALU.subtract, ALU.mult).then_inc(norm_done, 1)
                if name == "q":
                    r = phase_of(kind, s) % RING
                    b = bias_cols[:, QUERY_BIAS[kind]:QUERY_BIAS[kind] + CK]
                    dve.wait_ge(dense_ready, base + n + 1)
                    nc.vector.tensor_tensor(q_t[:, r], d[:, 0:C].rearrange("p (c t) -> p c t", t=P),
                                            b.unsqueeze(2).broadcast_to([P, CK, P]), ALU.add).then_inc(q_ready, 1)
                    dve.wait_ge(q_ready, i * COUNT["q"] + m + 1)
                    dve.sem_inc(dense_free[n % 2], 1)
                if name == "kv":
                    r = phase_of(kind, s) % RING
                    b = bias_cols[:, KEY_BIAS[kind]:KEY_BIAS[kind] + CK]
                    if m >= 3:
                        old = phase_of(*KV_ORDER[m - 3])
                        dve.wait_ge(k_placed[old % RING], i * FILLS * 16 * HC + 16 * HC * (old // RING + 1))
                    dve.wait_ge(dense_ready, base + n + 1)
                    nc.vector.tensor_tensor(k_t[:, m % 3], d[:, 0:C].rearrange("p (c t) -> p c t", t=P),
                                            b.unsqueeze(2).broadcast_to([P, CK, P]), ALU.add).then_inc(k_ready, 1)
                    v = v_pad[:, r].rearrange("p g a j -> p (g a j)").rearrange("p (g w) -> p g w", w=64)
                    for odd in range(2):
                        src = d[:, C:2 * C].rearrange("p (g a j) -> p g a j", a=2, j=D)[:, :, odd]
                        bv = b_value[:, kind].rearrange("p (g a j) -> p g a j", a=2, j=D)[:, :, odd]
                        e = nc.vector.tensor_tensor(v[:, :, 48 * odd:48 * odd + D], src, bv, ALU.add)
                    e.then_inc(v_ready, 1)
                    dve.wait_ge(v_ready, i * COUNT["kv"] + m + 1)
                    dve.sem_inc(dense_free[n % 2], 1)
                if name == "out":
                    dve.wait_ge(dense_ready, base + n + 1)
                    skip = i * COUNT["skip"] + NTH["skip", kind, s] + 1
                    if kind == LAST:
                        dve.wait_ge(skip_ready, skip)
                        nc.vector.tensor_tensor(x_mid[:, s, :], d[:, 0:C], x_skip[:, s, :],
                                                ALU.add).then_inc(x_done, 1)
                        dve.wait_ge(x_done, i * N_OUT + m + 1)
                        dve.sem_inc(dense_free[n % 2], 1)
                    else:
                        g = gates[:, s, GATE[kind] * C:(GATE[kind] + 1) * C]
                        dve.wait_ge(gates_loaded[s], (i + 1) * 16)
                        nc.vector.tensor_tensor(gated[:], d[:, 0:C], g, ALU.mult).then_inc(dense_free[n % 2], 1)
                        dve.wait_ge(dense_free[n % 2], half + n // 2 + 2)
                        dve.wait_ge(skip_ready, skip)
                        if kind == SELF:
                            dve.wait_ge(y_gone, i + 1)
                        nc.vector.tensor_tensor(x_mid[:, s, :], gated[:], x_skip[:, s, :],
                                                ALU.add).then_inc(x_done, 1)
                if name == "up":
                    dve.wait_ge(dense_ready, base + n + 1)
                    b = bias_cols[:, 38 + 4 * kind:42 + 4 * kind]
                    nc.vector.tensor_tensor(half_a[:, m % 2], d[:].rearrange("p (j t) -> p j t", t=P),
                                            b.unsqueeze(2).broadcast_to([P, 4, P]), ALU.add).then_inc(half_a_done, 1)
                    dve.wait_ge(half_a_done, i * COUNT["up"] + m + 1)
                    dve.sem_inc(dense_free[n % 2], 1)
                if name == "glu":
                    dve.wait_ge(tanh_done, i * COUNT["glu"] + m + 1)
                    nc.vector.scalar_tensor_tensor(
                        out=tanh_a[:, m % 2].rearrange("p j t -> p (j t)"),
                        in0=tanh_a[:, m % 2].rearrange("p j t -> p (j t)"), scalar=1.0,
                        in1=half_a[:, m % 2].rearrange("p j t -> p (j t)"),
                        op0=ALU.add, op1=ALU.mult).then_inc(silu_done, 1)

            def dense_parts(i, t, more, early):
                for part in PLAN.get(t, ()):
                    if (part[0] in EARLY) == early:
                        dense_part(part, i, N_FIRST + i * N_DENSE, N_FIRST // 2 + i * (N_DENSE // 2),
                                   (DENSE if more else DENSE_LAST)[part])
                for part in AHEAD.get(t, ()) if more else ():
                    if (part[0] in EARLY) == early:
                        dense_part(part, i + 1, N_FIRST + i * N_DENSE, N_FIRST // 2 + i * (N_DENSE // 2), DENSE[part])

            def body(i, more):
                for t in STEPS:
                    dense_parts(i, t, more, True)
                    u = t - O_LAG
                    if 0 <= u < UNITS and u % 4 == 3:
                        ph = u // 4
                        dve.wait_ge(o_ready, i * PHASES + ph + 1)
                        nc.vector.reciprocal(inv_sum[:], o_view[:, :, 1]).then_inc(inv_done, 1)
                        dve.wait_ge(inv_done, i * PHASES + ph + 1)
                        nc.vector.tensor_tensor(o_t[:], o_view[:, :, 0], inv_sum[:], ALU.mult).then_inc(o_t_ready, 1)
                    if 0 <= t < UNITS:
                        dve.wait_ge(scores_ready, i * UNITS + t + 1)
                        dve.sem_inc(dve_passed, 1)
                        if t // (4 * SLOTS) == CROSS:
                            top_k(i, t)
                        else:
                            nc.vector.tensor_reduce(neg_max[:, t % 4], score_bank[t % 3][:].rearrange("p (h t) -> p h t", t=P),
                                                    AX.X, ALU.max, negate=True).then_inc(scored, 1)
                    dense_parts(i, t, more, False)

            for t in sorted(AHEAD):
                for part in AHEAD[t]:
                    dense_part(part, 0, 0, 0, DENSE_FIRST[part])
            with dve.Fori(0, ITERS - 1) as i:
                body(i, True)
            body(ITERS - 1, False)


        @block.tensor
        def _(pe):
            pe.wait_ge(consts_ready, 1)
            pe.wait_ge(rows_loaded, 9 * 16)
            nc.tensor.transpose(dense_bank[0][:, 0:NBIAS], bias_rows[:], ident[0:NBIAS, 0:NBIAS]).then_inc(setup_pe, 1)
            pe.wait_ge(setup_dve, 2)
            for c in range(CK):
                e = nc.tensor.transpose(dense_bank[1][:, B * c:B * c + B], cond_silu[:, P * c:P * c + P], ident[0:B, 0:B])
            e.then_inc(setup_pe, 1)
            pe.wait_ge(ada_loaded, 3 * 16)
            pe.wait_ge(setup_dve, 5)
            cols = []
            for k in range(3):
                cols += [w_ada[:, :, C * (3 * k + 1) + P * c:C * (3 * k + 1) + P * c + P] for c in range(CK)]
                cols += [w_ada[:, :, C * 3 * k + P * c:C * 3 * k + P * c + P] for c in range(CK)]
            for w in (ss_q, ss_kv):
                cols += [w[:, :, P * c:P * c + P] for c in range(4)]
            for j, w in enumerate(cols):
                for c in range(CK):
                    e = nc.tensor.matmul(score_bank[0][:, B * j:B * j + B], w[:, c], silu_t[:, c],
                                         start=(c == 0), stop=(c == CK - 1))
            e.then_inc(setup_pe, 1)
            for k in range(3):
                dst = score_bank[1][0:B, C * k:C * k + C] if k < 2 else score_bank[2][0:B, 0:C]
                for c in range(CK):
                    e = nc.tensor.matmul(dst, silu_t[:, c], w_ada[:, c, C * (3 * k + 2):C * (3 * k + 3)],
                                         start=(c == 0), stop=(c == CK - 1))
            e.then_inc(setup_pe, 1)
            for w in w_loaded.values():
                pe.wait_ge(w, 16)
            pe.wait_ge(w_scaled, 4)
            pe.wait_ge(consts_ready, 2)
            pe.wait_ge(setup_dve, 8)

            def dense_part(part, i, base, half, n_dense):
                name, kind, s = part
                n = n_dense
                d = dense_bank[n % 2]
                if name in DENSE_USES:
                    pe.wait_ge(dense_free[n % 2], half + n // 2 + 1)
                if name == "turn":
                    pe.wait_ge(norm_done, i * COUNT["norm"] + NTH["norm", kind, s] + 1)
                    g = NTH["norm", kind, s] % 3
                    for c in range(CK):
                        e = nc.tensor.transpose(d[:, P * c:P * c + P], x_norm[:, g, P * c:P * c + P], ident[:])
                    e.then_inc(dense_ready, 1)
                if name == "turn_ctx":
                    pe.wait_ge(norm_done, i * COUNT["norm"] + NTH["norm", kind, s] + 1)
                    g = NTH["norm", kind, s] % 3
                    for c in range(CK):
                        nc.tensor.transpose(d[:, P * c:P * c + P], ctx_in[:, s, P * c:P * c + P], ident[:])
                    for c in range(CK):
                        e = nc.tensor.transpose(d[:, P * (2 + c):P * (3 + c)], x_norm[:, g, P * c:P * c + P], ident[:])
                    e.then_inc(dense_ready, 1)
                if name == "q":
                    pe.wait_ge(h_ready, (i * COUNT["turn"] + NTH["turn", kind, s] + 1) * 2)
                    for j in range(CK):
                        for c in range(CK):
                            e = nc.tensor.matmul(d[:, P * j:P * j + P], w_query[kind][:, c, P * j:P * j + P],
                                                 h_t[:, s, c], start=(c == 0), stop=(c == CK - 1))
                    e.then_inc(dense_ready, 1)
                if name == "kv":
                    src = {SELF: h_t[:, s], CROSS: ctx_t[:, 0], LAST: ctx_norm_t[:, s % 3]}[kind]
                    turn = ("turn", SELF, s) if kind == SELF else ("turn_ctx", CTX, s)
                    pe.wait_ge(h_ready, (i * COUNT["turn"] + NTH[turn] + 1) * 2)
                    for j in range(CK):
                        for c in range(CK):
                            nc.tensor.matmul(d[:, P * j:P * j + P], w_key[kind][:, c, P * j:P * j + P],
                                             src[:, c], start=(c == 0), stop=(c == CK - 1))
                    for c in range(CK):
                        e = nc.tensor.matmul(d[:, C:2 * C], src[:, c], w_value[kind][:, c],
                                             start=(c == 0), stop=(c == CK - 1))
                    e.then_inc(dense_ready, 1)
                if name == "out" and kind != MLP:
                    pe.wait_ge(o_t_ready, i * PHASES + phase_of(kind, s) + 1)
                    for c in range(CK):
                        e = nc.tensor.matmul(d[:, 0:C], o_t[:, c], w_out[kind][:, c],
                                             start=(c == 0), stop=(c == CK - 1))
                    e.then_inc(dense_ready, 1)
                if name == "up":
                    if kind == 0:
                        pe.wait_ge(h_ready, (i * COUNT["turn"] + NTH["turn", MLP, s] + 1) * 2)
                    for lin in range(2):
                        d = dense_bank[(n + lin) % 2]
                        if lin:
                            pe.wait_ge(dense_free[(n + 1) % 2], half + (n + 1) // 2 + 1)
                        for j in range(4):
                            at = HID * lin + P * (4 * kind + j)
                            for c in range(CK):
                                e = nc.tensor.matmul(d[:, P * j:P * j + P], w_m1[:, c, at:at + P], h_t[:, s, c],
                                                     start=(c == 0), stop=(c == CK - 1))
                        e.then_inc(dense_ready, 1)
                if name == "out" and kind == MLP:
                    for j in range(HB):
                        if j % 4 == 0:
                            pe.wait_ge(glu_done, i * COUNT["glu"] + NTH["glu", j // 4, s] + 1)
                        e = nc.tensor.matmul(d[:, 0:C], glu[:, j], w_m2[:, j],
                                             start=(j == 0), stop=(j == HB - 1))
                    e.then_inc(dense_ready, 1)

            def dense_parts(i, t, more):
                for part in PLAN.get(t, ()):
                    dense_part(part, i, N_FIRST + i * N_DENSE, N_FIRST // 2 + i * (N_DENSE // 2),
                               (DENSE if more else DENSE_LAST)[part])
                for part in AHEAD.get(t, ()) if more else ():
                    dense_part(part, i + 1, N_FIRST + i * N_DENSE, N_FIRST // 2 + i * (N_DENSE // 2), DENSE[part])

            def body(i, more):
                for t in STEPS:
                    u = t - TURN_LAG
                    if 0 <= u < UNITS:
                        if u // (4 * SLOTS) == CROSS:
                            pe.wait_ge(top_ready, i * 4 * SLOTS + u - 4 * SLOTS + 1)
                            src = left
                        else:
                            pe.wait_ge(probs_ready, i * UNITS + u + 1)
                            src = probs
                        for h in range(QH):
                            e = nc.tensor.transpose(turn_bank[u % 2][:, P * h:P * h + P], src[:, u % 4, h], ident[:])
                        e.then_inc(turned, 1)
                    u = t + SCORE_AHEAD
                    if 0 <= u < UNITS:
                        ph, c, blk = u // 4, u % 4 // 2, 4 * (u % 2)
                        kind, s, r = ph // SLOTS, ph % SLOTS, ph % RING
                        if u % 4 == 0:
                            pe.wait_ge(q_ready, i * COUNT["q"] + NTH["q", kind, s] + 1)
                            pe.wait_ge(k_placed[r], i * FILLS * 16 * HC + 16 * HC * (ph // RING + 1))
                        if u >= 3:
                            pe.wait_ge(probs_ready, i * UNITS + u - 2)
                        nc.tensor.matmul(score_bank[u % 3][:], q_t[:, r, c],
                                         k_blocks[:, r, c, blk:blk + 4].rearrange("p h t -> p (h t)"),
                                         start=True, stop=True).then_inc(scores_ready, 1)
                    dense_parts(i, t, more)
                    u = t - SUM_LAG
                    if 0 <= u < UNITS:
                        ph, c = u // 4, u % 4 // 2
                        kind, s, r = ph // SLOTS, ph % SLOTS, ph % RING
                        if u % 4 == 0:
                            pe.wait_ge(v_ready, i * COUNT["kv"] + NTH["kv", kind, s] + 1)
                            if ph:
                                pe.wait_ge(o_t_ready, i * PHASES + ph)
                        pe.wait_ge(probs_t_ready, i * UNITS + u + 1)
                        for what in range(2):
                            for g in range(2):
                                lane = 32 * (2 * (u % 2) + g)
                                for odd in range(2):
                                    w = v_pad[:, r, 2 * (u % 4) + g, odd] if what == 0 else one_cols[:, odd]
                                    e = nc.tensor.matmul(o_view[lane:lane + 32, c, what], w, probs_t[:, u % 3, 2 * g + odd],
                                                         start=(odd == 0), stop=(odd == 1))
                        if u % 4 == 3:
                            e.then_inc(o_ready, 1)

            for t in sorted(AHEAD):
                for part in AHEAD[t]:
                    dense_part(part, 0, 0, 0, DENSE_FIRST[part])
            with pe.Fori(0, ITERS - 1) as i:
                body(i, True)
            body(ITERS - 1, False)



PLAN_SKIPS_LAST = [NTH["skip", LAST, s] for s in range(SLOTS)]

_INS = ["x", "cond_1024", "ctx_1024", "L0_xcond_w_ada", "L0_xcond_b_ada", "L0_xcond_w_qkv", "L0_xcond_b_qkv",
        "L0_xcond_w_so", "L0_xcond_b_so", "L0_xcond_w_q", "L0_xcond_b_q", "L0_xcond_w_kv", "L0_xcond_b_kv",
        "L0_xcond_w_co", "L0_xcond_b_co", "L0_xcond_w_m1", "L0_xcond_b_m1", "L0_xcond_w_m2", "L0_xcond_b_m2",
        "L1_xcond_Wq", "L1_xcond_bq", "L1_xcond_Wkv", "L1_xcond_bkv", "L1_xcond_Wp", "L1_xcond_bp",
        "L1_xcond_Wss_q", "L1_xcond_bss_q", "L1_xcond_Wss_kv", "L1_xcond_bss_kv"]


def kernel(**inputs):
    import numpy as np
    import concourse.bacc as bacc
    from concourse import mybir as _mybir
    from concourse.bass_utils import run_bass_kernel_spmd

    nc = bacc.Bacc("TRN2", target_bir_lowering=False, num_devices=1)
    arrays, aps = {}, {}
    for name in _INS:
        arr = np.ascontiguousarray(inputs[name])
        arrays[f"in_{name}"] = arr
        aps[name] = nc.dram_tensor(f"in_{name}", arr.shape, _mybir.dt.from_np(arr.dtype), kind="ExternalInput").ap()
    out = nc.dram_tensor("out_y", (B, P, C), F32, kind="ExternalOutput").ap()
    block_kernel(nc, aps, out)
    r = run_bass_kernel_spmd(nc, [arrays], core_ids=[0])
    return r.results[0]["out_y"]
```

```python
from contextlib import ExitStack

import concourse.bass as bass
from concourse import mybir

F32 = mybir.dt.float32
ALU = mybir.AluOpType
ACT = mybir.ActivationFunctionType
AX = mybir.AxisListType

P = 128
B = 16
C = 256
CK = C // P
H = 16
D = C // H
HC = P // D
HID = 1024
HB = HID // P
SLOTS = 4
ITERS = B // SLOTS
QH = 4
PHASES = 3 * SLOTS
UNITS = PHASES * (H // QH)
RING = 6
FILLS = PHASES // RING
GONE = -(2.0 ** 127)

SELF, CROSS, LAST, MLP, CTX = range(5)
LNS = {SELF: 1e-6, CROSS: 1e-6, MLP: 1e-6, LAST: 1e-5, CTX: 1e-5}
NMOD = 4 * len(LNS)
NBIAS = 18 + 4 + 4 + 4 + 2 + 2 + 2 + 2 + 16

SCORE_AHEAD, TURN_LAG, SUM_LAG, O_LAG = 1, 3, 4, 5
SCORE_BANKS, TURN_BANKS, DENSE_BANKS = 3, 2, 2


EARLY, ON_TIME, LATE = range(3)


def dve_order(part):
    if part[0] in ("norm", "glu"):
        return EARLY
    return LATE if part[0] == "kv" or part[:2] == ("out", SELF) or part[0] == "q" and part[1] != LAST else ON_TIME



PLAN, AHEAD = {}, {}


def _put(step, *part):
    if step < 0:
        AHEAD.setdefault(step + UNITS, []).append(part)
    else:
        PLAN.setdefault(step, []).append(part)


for _s in range(SLOTS):
    _first = 4 * _s
    for _step, *_part in (
            (-8, "stats", SELF), (-6, "norm", SELF), (-6, "turn", SELF), (-5, "kv", SELF), (-5, "q", SELF),
            (3, "skip", SELF), (8, "out", SELF), (9, "stats", CROSS), (10, "skip", CROSS), (11, "norm", CROSS),
            (11, "turn", CROSS), (12, "q", CROSS), (5, "stats", CTX),
            (7, "norm", CTX), (7, "turn_ctx", CTX), (10, "kv", CROSS), (18, "kv", LAST)):
        _put(_first + _step, *_part, _s)
    _first += 4 * SLOTS
    for _step, *_part in (
            (8, "out", CROSS), (8, "stats", MLP), (9, "norm", MLP), (9, "turn", MLP), (9, "skip", MLP),
            (10, "up", 0), (11, "glu", 0), (11, "up", 1), (12, "glu", 1), (12, "out", MLP),
            (12, "stats", LAST), (13, "norm", LAST), (13, "turn", LAST), (13, "skip", LAST),
            (14, "q", LAST), (24, "out", LAST)):
        _put(_first + _step, *_part, _s)
STEPS = range(-SCORE_AHEAD, max(max(PLAN), UNITS + O_LAG - 1) + 1)

DENSE_USES = {"q": 1, "kv": 1, "turn": 1, "turn_ctx": 1, "out": 1, "up": 2}
NTH, COUNT = {}, {}
for _plan in (AHEAD, PLAN):
    for _t in sorted(_plan):
        for _part in _plan[_t]:
            _sort = {"turn_ctx": "turn"}.get(_part[0], _part[0])
            NTH[_part] = COUNT.get(_sort, 0)
            COUNT[_sort] = NTH[_part] + 1
for _t in sorted(AHEAD):
    for _part in AHEAD[_t]:
        for _u in PLAN:
            for _other in PLAN[_u]:
                assert _u <= _t or _other[0].split("_")[0] != _part[0].split("_")[0], (_part, _other)
DENSE, DENSE_FIRST, N_DENSE, N_FIRST = {}, {}, 0, 0
for _t in sorted(AHEAD):
    for _part in AHEAD[_t]:
        DENSE_FIRST[_part] = N_FIRST
        N_FIRST += DENSE_USES.get(_part[0], 0)
for _t in STEPS:
    for _part in PLAN.get(_t, []) + AHEAD.get(_t, []):
        DENSE[_part] = N_FIRST + N_DENSE
        N_DENSE += DENSE_USES.get(_part[0], 0)
DENSE_LAST, _n = {}, N_FIRST
for _t in STEPS:
    for _part in PLAN.get(_t, []):
        DENSE_LAST[_part] = _n
        _n += DENSE_USES.get(_part[0], 0)
assert N_DENSE % DENSE_BANKS == 0
GATE = {SELF: 0, CROSS: 1, MLP: 2}
N_OUT = COUNT["out"]
WEIGHTS = {("out", SELF): ("so",), ("kv", CROSS): ("kv",), ("q", CROSS): ("q",), ("out", CROSS): ("co",),
           ("up", 0): ("m1",), ("out", MLP): ("m2",), ("kv", LAST): ("lkv",), ("q", LAST): ("lq",),
           ("out", LAST): ("lp",)}
SCALED = {("q", CROSS): 2, ("q", LAST): 3}
KV_ORDER = [part[1:] for part in sorted((q for q in NTH if q[0] == "kv"), key=NTH.get)]
QUERY_BIAS = {SELF: 26, CROSS: 30, LAST: 34}
KEY_BIAS = {SELF: 28, CROSS: 32, LAST: 36}


def block_kernel(nc, a, out):
    with ExitStack() as ctx:
        def sb(name, *shape):
            return ctx.enter_context(nc.sbuf_tensor(name, list(shape), F32))

        def bank(name):
            return ctx.enter_context(nc.psum_tensor(name, [P, 512], F32))

        def sem(name):
            return ctx.enter_context(nc.semaphore(name))

        w_qkv = sb("w_qkv", P, CK, 3 * C)
        w_so = sb("w_so", P, CK, C)
        w_q = sb("w_q", P, CK, C)
        w_kv = sb("w_kv", P, CK, 2 * C)
        w_co = sb("w_co", P, CK, C)
        w_m1 = sb("w_m1", P, CK, 2 * HID)
        w_m2 = sb("w_m2", P, HB, C)
        l_q = sb("l_q", P, CK, C)
        l_kv = sb("l_kv", P, CK, 2 * C)
        l_p = sb("l_p", P, CK, C)
        w_query = {SELF: w_qkv[:, :, 0:C], CROSS: w_q[:], LAST: l_q[:]}
        w_key = {SELF: w_qkv[:, :, C:2 * C], CROSS: w_kv[:, :, 0:C], LAST: l_kv[:, :, 0:C]}
        w_value = {SELF: w_qkv[:, :, 2 * C:3 * C], CROSS: w_kv[:, :, C:2 * C], LAST: l_kv[:, :, C:2 * C]}
        w_out = {SELF: w_so, CROSS: w_co, LAST: l_p}
        b_value = sb("b_value", P, 3, C)
        b_out = sb("b_out", P, 4, C)
        bias_rows = sb("bias_rows", NBIAS, P)
        bias_cols = sb("bias_cols", P, NBIAS)
        mod_bias = sb("mod_bias", P, NMOD)
        silu_t = sb("silu_t", P, CK, B)
        mod_all = sb("mod_all", P, B, NMOD)
        mod_now = sb("mod_now", P, SLOTS, NMOD)
        ident = sb("ident", P, P)
        minus_half = sb("minus_half", P, 1)
        one_cols = sb("one_cols", P, 2, 32)
        x_in = sb("x_in", P, SLOTS, C)
        ctx_in = sb("ctx_in", P, SLOTS, C)
        gates = sb("gates", P, SLOTS, 3 * C)
        x_mid = sb("x_mid", P, SLOTS, C)
        x_skip = sb("x_skip", P, SLOTS, C)
        gated = sb("gated", P, C)
        x_norm = sb("x_norm", P, 3, C)
        ln_stats = sb("ln_stats", P, 4, 6)
        ln_mv = sb("ln_mv", P, 4, 2)
        ln_var = sb("ln_var", P, 4, 1)
        ln_rstd = sb("ln_rstd", P, 4, 1)
        h_t = sb("h_t", P, SLOTS, CK, P)
        ctx_t = sb("ctx_t", P, 1, CK, P)
        ctx_norm_t = sb("ctx_norm_t", P, 3, CK, P)
        q_t = sb("q_t", P, RING, CK, P)
        k_t = sb("k_t", P, 3, CK, P)
        k_blocks = sb("k_blocks", P, RING, CK, HC, P)
        v_pad = sb("v_pad", P, RING, H // 2, 2, 32)
        neg_max = sb("neg_max", P, 4, QH)
        row_sum = sb("row_sum", P, 4, QH)
        probs = sb("probs", P, 4, QH, P)
        left = sb("left", P, 4, QH, P)
        top8 = sb("top8", P, 2, QH, 8)
        probs_t = sb("probs_t", P, 3, QH, P)
        inv_sum = sb("inv_sum", P, CK, P)
        o_t = sb("o_t", P, CK, P)
        lin_a = sb("lin_a", P, 2, 4, P)
        tanh_a = sb("tanh_a", P, 2, 4, P)
        half_b = sb("half_b", P, 2, 4, P)
        glu = sb("glu", P, HB, P)
        gate_rows = glu[0:B].rearrange("p j t -> p (j t)")[:, 0:3 * C]
        gates_dram = nc.dram_tensor("gates_dram", (B, 3 * C), F32).ap()
        FIRST = 2
        arena = k_blocks[:, FIRST:].rearrange("p r c h t -> p (r c h t)")
        NADA = 9 * C
        w_ada = arena[:, 0:CK * NADA].rearrange("p (c n) -> p c n", c=CK)
        ss_q = arena[:, CK * NADA:CK * (NADA + 2 * C)].rearrange("p (c n) -> p c n", c=CK)
        ss_kv = arena[:, CK * (NADA + 2 * C):CK * (NADA + 4 * C)].rearrange("p (c n) -> p c n", c=CK)

        spare = arena[0:B, CK * (NADA + 4 * C):]
        gate_bias = spare[:, 0:3 * C]
        cond, cond_tanh, cond_silu = (spare[:, n * C:(n + 1) * C] for n in (3, 4, 5))

        score_bank = [bank(f"score_bank{n}") for n in range(SCORE_BANKS)]
        turn_bank = [bank(f"turn_bank{n}") for n in range(TURN_BANKS)]
        o_bank = bank("o_bank")
        dense_bank = [bank(f"dense_bank{n}") for n in range(DENSE_BANKS)]
        o_view = o_bank[:].rearrange("p (c k t) -> p c k t", c=CK, k=2)

        cond_loaded = sem("cond_loaded")
        ada_loaded = [sem(f"ada_loaded{k}") for k in range(3)]
        ss_loaded = sem("ss_loaded")
        rows_loaded = sem("rows_loaded")
        b_value_loaded = sem("b_value_loaded")
        b_out_loaded = sem("b_out_loaded")
        gate_bias_loaded = sem("gate_bias_loaded")
        w_loaded = {k: sem(f"w_loaded_{k}") for k in ("qkv", "so", "q", "kv", "co", "m1", "m2", "lq", "lkv", "lp")}
        x_loaded = [sem(f"x_loaded{s}") for s in range(SLOTS)]
        ctx_loaded = [sem(f"ctx_loaded{s}") for s in range(SLOTS)]
        gates_loaded = [sem(f"gates_loaded{s}") for s in range(SLOTS)]
        gates_stored = sem("gates_stored")
        k_placed = [sem(f"k_placed{r}") for r in range(RING)]
        y_stored = sem("y_stored")
        y_gone = sem("y_gone")
        ident_step = sem("ident_step")
        consts_ready = sem("consts_ready")
        blocks_zeroed = sem("blocks_zeroed")
        w_scaled = sem("w_scaled")
        setup_act = sem("setup_act")
        setup_dve = sem("setup_dve")
        setup_pe = sem("setup_pe")
        dve_passed = sem("dve_passed")
        pool_passed = sem("pool_passed")
        sp_passed = sem("sp_passed")
        mod_ready = sem("mod_ready")
        mod_rest_ready = sem("mod_rest_ready")
        bn_done = sem("bn_done")
        stats_done = sem("stats_done")
        var_done = sem("var_done")
        rstd_done = sem("rstd_done")
        norm_done = sem("norm_done")
        h_ready = sem("h_ready")
        q_ready = sem("q_ready")
        k_ready = sem("k_ready")
        v_ready = sem("v_ready")
        skip_part = sem("skip_part")
        skip_ready = sem("skip_ready")
        gated_done = sem("gated_done")
        x_done = sem("x_done")
        lin_a_done = sem("lin_a_done")
        tanh_done = sem("tanh_done")
        half_b_done = sem("half_b_done")
        silu_done = sem("silu_done")
        glu_done = sem("glu_done")
        dense_ready = sem("dense_ready")
        dense_free = [sem(f"dense_free{n}") for n in range(DENSE_BANKS)]
        scores_ready = sem("scores_ready")
        topk_step = sem("topk_step")
        scored = sem("scored")
        left_ready = sem("left_ready")
        probs_ready = sem("probs_ready")
        mask_done = sem("mask_done")
        inv_row_done = sem("inv_row_done")
        weights_ready = sem("weights_ready")
        turned = sem("turned")
        probs_t_ready = sem("probs_t_ready")
        o_ready = sem("o_ready")
        inv_done = sem("inv_done")
        o_t_ready = sem("o_t_ready")

        block = ctx.enter_context(nc.Block())

        def phase_of(kind, s):
            return SLOTS * kind + s

        @block.sync
        def _(sp):
            def chunks(w):
                return w.rearrange("(c p) n -> p c n", p=P)

            def rows(v):
                return v.rearrange("(c p) -> c p", p=P)

            sp.dma_start(cond, a["cond_1024"]).then_inc(cond_loaded, 16)
            at = 0
            for v in (a["L0_xcond_b_ada"], a["L1_xcond_bss_q"], a["L1_xcond_bss_kv"],
                      a["L0_xcond_b_qkv"][0:2 * C], a["L0_xcond_b_q"], a["L0_xcond_b_kv"][0:C],
                      a["L1_xcond_bq"], a["L1_xcond_bkv"][0:C], a["L0_xcond_b_m1"]):
                n = v.shape[0] // P
                sp.dma_start(bias_rows[at:at + n, :], rows(v)).then_inc(rows_loaded, 16)
                at += n
            for k in range(3):
                cols = slice(3 * C * k, 3 * C * (k + 1))
                sp.dma_start(w_ada[:, :, cols], chunks(a["L0_xcond_w_ada"])[:, :, cols]).then_inc(ada_loaded[k], 16)
                if k == 0:
                    for s in range(FIRST):
                        sp.dma_start(x_in[:, s, :], a["x"][s]).then_inc(x_loaded[s], 16)
                    sp.dma_start(w_qkv[:], chunks(a["L0_xcond_w_qkv"])).then_inc(w_loaded["qkv"], 16)
                    for n, v in enumerate((a["L0_xcond_b_qkv"][2 * C:3 * C], a["L0_xcond_b_kv"][C:2 * C],
                                           a["L1_xcond_bkv"][C:2 * C])):
                        sp.dma_start(b_value[:, n, :], v.partition_broadcast(P)).then_inc(b_value_loaded, 16)
            sp.dma_start(ss_q, chunks(a["L1_xcond_Wss_q"])).then_inc(ss_loaded, 16)
            sp.dma_start(ss_kv, chunks(a["L1_xcond_Wss_kv"])).then_inc(ss_loaded, 16)
            gate_chunks = a["L0_xcond_b_ada"].rearrange("(k n) -> k n", n=C)[2::3]
            sp.dma_start(gate_bias.rearrange("b (k n) -> b k n", n=C),
                         gate_chunks.partition_broadcast(B)).then_inc(gate_bias_loaded, 16)

            def place_k(part, i):
                r = phase_of(*part[1:]) % RING
                sp.wait_ge(k_ready, i * COUNT["kv"] + NTH[part] + 1)
                for h in range(HC):
                    rows_h = slice(D * h, D * h + D)
                    sp.dma_start(k_blocks[rows_h, r, :, h, :], k_t[rows_h, NTH[part] % 3]).then_inc(k_placed[r], 16)

            for s in range(FIRST, SLOTS):
                sp.dma_start(x_in[:, s, :], a["x"][s]).then_inc(x_loaded[s], 16)
            for s in range(SLOTS):
                sp.dma_start(ctx_in[:, s, :], a["ctx_1024"][s]).then_inc(ctx_loaded[s], 16)
            for key, dst, src in (("kv", w_kv, "L0_xcond_w_kv"), ("so", w_so, "L0_xcond_w_so"),
                                  ("q", w_q, "L0_xcond_w_q"), ("lq", l_q, "L1_xcond_Wq")):
                sp.dma_start(dst[:], chunks(a[src])).then_inc(w_loaded[key], 16)
            sp.wait_ge(blocks_zeroed, 1)
            for t in sorted(AHEAD):
                for part in AHEAD[t]:
                    if part[0] == "kv":
                        place_k(part, 0)
            for n, v in enumerate((a["L0_xcond_b_so"], a["L0_xcond_b_co"], a["L1_xcond_bp"],
                                   a["L0_xcond_b_m2"])):
                sp.dma_start(b_out[:, n, :], v.partition_broadcast(P)).then_inc(b_out_loaded, 16)
            for key, dst, src in (("lkv", l_kv, "L1_xcond_Wkv"),
                                  ("m1", w_m1, "L0_xcond_w_m1"), ("co", w_co, "L0_xcond_w_co"),
                                  ("m2", w_m2, "L0_xcond_w_m2"), ("lp", l_p, "L1_xcond_Wp")):
                sp.dma_start(dst[:], chunks(a[src])).then_inc(w_loaded[key], 16)
            sp.wait_ge(setup_dve, 9)
            sp.dma_start(gates_dram, gate_rows).then_inc(gates_stored, 16)
            sp.wait_ge(gates_stored, 16)
            for s in range(SLOTS):
                sp.dma_start(gates[:, s, :], gates_dram[s].partition_broadcast(P)).then_inc(gates_loaded[s], 16)
            sp.sem_inc(y_gone, 1)
            sp.wait_ge(blocks_zeroed, 4)

            def body(i, more):
                for t in STEPS:
                    for part in PLAN.get(t, ()):
                        name, kind, s = part
                        nxt = (i + 1) * SLOTS + s
                        if name == "kv":
                            place_k(part, i)
                            if kind == CROSS and more:
                                sp.dma_start(ctx_in[:, s, :], a["ctx_1024"][nxt]).then_inc(ctx_loaded[s], 16)
                        if name == "out":
                            if kind == LAST or more:
                                sp.wait_ge(x_done, i * N_OUT + NTH[part] + 1)
                                sp.sem_inc(sp_passed, 1)
                            if kind == LAST:
                                sp.dma_start(out[i * SLOTS + s], x_mid[:, s, :]).then_inc(y_stored, 16)
                            if kind == SELF and more:
                                sp.dma_start(x_in[:, s, :], a["x"][nxt]).then_inc(x_loaded[s], 16)
                            if kind == MLP and more:
                                sp.dma_start(gates[:, s, :], gates_dram[nxt].partition_broadcast(P)).then_inc(gates_loaded[s], 16)
                    for part in AHEAD.get(t, ()) if more else ():
                        if part[0] == "kv":
                            place_k(part, i + 1)
                sp.wait_ge(y_stored, (i + 1) * 16 * SLOTS)
                sp.sem_inc(y_gone, 1)

            with sp.Fori(0, ITERS - 1) as i:
                body(i, True)
            body(ITERS - 1, False)

        @block.gpsimd
        def _(pool):
            nc.gpsimd.memset(ident[:], 0.0).then_inc(ident_step, 1)
            pool.wait_ge(ident_step, 1)
            nc.gpsimd.affine_select(out=ident[:], in_=ident[:], compare_op=ALU.not_equal, fill=1.0,
                                    base=0, pattern=[[-1, P]], channel_multiplier=1).then_inc(consts_ready, 1)
            nc.gpsimd.memset(minus_half[:], -0.5)
            nc.gpsimd.memset(v_pad[:], 0.0)
            nc.gpsimd.memset(one_cols[:], 0.0).then_inc(ident_step, 1)
            pool.wait_ge(ident_step, 2)
            nc.gpsimd.memset(one_cols[:, 0, 0:D], 1.0)
            nc.gpsimd.memset(one_cols[:, 1, D:2 * D], 1.0).then_inc(consts_ready, 1)
            nc.gpsimd.memset(k_blocks[:, 0:FIRST], 0.0).then_inc(blocks_zeroed, 1)

            def scale_query(kind):
                key, w = {SELF: "qkv", CROSS: "q", LAST: "lq"}[kind], w_query[kind]
                pool.wait_ge(w_loaded[key], 16)
                nc.gpsimd.tensor_scalar(w, w, 0.25, 1.0, ALU.mult, ALU.mult).then_inc(w_scaled, 1)

            pool.wait_ge(consts_ready, 2)
            scale_query(SELF)

            def dense_part(part, i, base, round_, n_dense):
                name, kind, s = part
                n = NTH[part]
                if name == "stats":
                    pool.wait_ge(stats_done, i * COUNT["stats"] + n + 1)
                    pool.sem_inc(pool_passed, 1)
                    nc.gpsimd.tensor_scalar(ln_var[:, n % 4], ln_mv[:, n % 4, 1:2], LNS[kind], 1.0,
                                            ALU.add, ALU.mult).then_inc(var_done, 1)
                    pool.wait_ge(var_done, i * COUNT["stats"] + n + 1)
                    nc.gpsimd.tensor_tensor(ln_rstd[:, n % 4], ln_var[:, n % 4], minus_half[:],
                                            ALU.pow).then_inc(rstd_done, 1)
                if name == "skip":
                    x_old = x_in if kind == SELF else x_mid
                    if kind == SELF:
                        pool.wait_ge(x_loaded[s], (i + 1) * 16)
                        pool.wait_ge(gates_loaded[s], (i + 1) * 16)
                    else:
                        before = {CROSS: SELF, MLP: CROSS, LAST: MLP}[kind]
                        pool.wait_ge(x_done, i * N_OUT + NTH["out", before, s] + 1)
                    bias = b_out[:, {SELF: 0, CROSS: 1, LAST: 2, MLP: 3}[kind], :]
                    if s == 0:
                        pool.wait_ge(b_out_loaded, 4 * 16)
                    if kind in GATE:
                        g = gates[:, s, GATE[kind] * C:(GATE[kind] + 1) * C]
                        nc.gpsimd.tensor_tensor(x_skip[:, s, :], bias, g, ALU.mult).then_inc(skip_part, 1)
                        m = n - sum(1 for q in PLAN_SKIPS_LAST if q < n)
                        pool.wait_ge(skip_part, i * (COUNT["skip"] - SLOTS) + m + 1)
                        bias = x_skip[:, s, :]
                    nc.gpsimd.tensor_tensor(x_skip[:, s, :], x_old[:, s, :], bias,
                                            ALU.add).then_inc(skip_ready, 1)
                if name == "glu":
                    pool.wait_ge(silu_done, i * COUNT["glu"] + n + 1)
                    pool.wait_ge(half_b_done, i * COUNT["glu"] + n + 1)
                    nc.gpsimd.tensor_tensor(glu[:, 4 * kind:4 * kind + 4], tanh_a[:, n % 2],
                                            half_b[:, n % 2], ALU.mult).then_inc(glu_done, 1)

            def dense_parts(i, t, more, early):
                for part in PLAN.get(t, ()):
                    if (part[0] in ("stats", "glu")) == early:
                        dense_part(part, i, i * N_DENSE, i * (N_DENSE // DENSE_BANKS),
                                   (DENSE if more else DENSE_LAST)[part])
                for part in AHEAD.get(t, ()) if more else ():
                    if (part[0] in ("stats", "glu")) == early:
                        dense_part(part, i + 1, i * N_DENSE, i * (N_DENSE // DENSE_BANKS), DENSE[part])

            def body(i, more):
                for t in STEPS:
                    dense_parts(i, t, more, True)
                    u = t - 1
                    if 0 <= u < UNITS and u // (4 * SLOTS) != CROSS:
                        n = u if u < 4 * SLOTS else u - 4 * SLOTS
                        pool.wait_ge(inv_row_done, i * (UNITS - 4 * SLOTS) + n + 1)
                        nc.gpsimd.tensor_tensor(probs[:, u % 4], probs[:, u % 4],
                                                row_sum[:, u % 4].unsqueeze(2).broadcast_to([P, QH, P]),
                                                ALU.mult).then_inc(weights_ready, 1)
                    if 0 <= t < UNITS and SLOTS * 4 <= t < 2 * SLOTS * 4:
                        n = t - SLOTS * 4
                        pool.wait_ge(left_ready, i * 4 * SLOTS + n + 1)
                        pool.sem_inc(pool_passed, 1)
                        nc.gpsimd.tensor_scalar(left[:, t % 4], left[:, t % 4], GONE, None,
                                                ALU.is_equal).then_inc(mask_done, 1)
                        pool.wait_ge(mask_done, i * 4 * SLOTS + n + 1)
                        pool.wait_ge(probs_ready, i * UNITS + t + 1)
                        nc.gpsimd.tensor_tensor(left[:, t % 4], left[:, t % 4], probs[:, t % 4],
                                                ALU.mult).then_inc(weights_ready, 1)
                    dense_parts(i, t, more, False)

            for t in sorted(AHEAD):
                for part in AHEAD[t]:
                    dense_part(part, 0, 0, 0, DENSE_FIRST[part])
            scale_query(CROSS)
            pool.wait_ge(setup_dve, 9)
            nc.gpsimd.memset(k_blocks[:, FIRST:FIRST + 2], 0.0).then_inc(blocks_zeroed, 1)
            scale_query(LAST)
            with pool.Fori(0, ITERS - 1) as i:
                body(i, True)
            body(ITERS - 1, False)


        @block.scalar
        def _(act):
            act.wait_ge(cond_loaded, 16)
            nc.scalar.activation(cond_tanh, cond, ACT.Tanh, scale=0.5).then_inc(setup_act, 1)
            def dense_part(part, i, base, round_, n_dense):
                name, kind, s = part
                n = n_dense
                if name in ("turn", "turn_ctx"):
                    if (name, kind) == ("turn", SELF):
                        act.wait_ge(mod_ready, i * SLOTS + s + 1)
                    if name == "turn_ctx":
                        act.wait_ge(mod_rest_ready, i * SLOTS + s + 1)
                    act.wait_ge(dense_ready, base + n + 1)
                    d = dense_bank[n % DENSE_BANKS]
                    dst, at = (h_t[:, s], 0) if name == "turn" else (ctx_norm_t[:, s % 3], 2 * P)
                    if name == "turn_ctx":
                        nc.scalar.copy(ctx_t[:, 0].rearrange("p c t -> p (c t)"), d[:, 0:2 * P])
                    ln = {SELF: 0, CROSS: 1, MLP: 2, LAST: 3, CTX: 4}[kind]
                    for c in range(CK):
                        e = nc.scalar.activation(dst[:, c], d[:, at + P * c:at + P * c + P], ACT.Identity,
                                                 scale=mod_now[:, s, 4 * ln + c:4 * ln + c + 1],
                                                 bias=mod_now[:, s, 4 * ln + 2 + c:4 * ln + 3 + c])
                        if c == 0:
                            e.then_inc(h_ready, 1)
                    e.then_inc(h_ready, 1)
                    act.wait_ge(h_ready, i * 2 * COUNT["turn"] + 2 * NTH[part] + 2)
                    act.sem_inc(dense_free[n % DENSE_BANKS], 1)
                if name == "up":
                    m = NTH[part]
                    act.wait_ge(lin_a_done, i * COUNT["up"] + m + 1)
                    nc.scalar.activation(tanh_a[:, m % 2], lin_a[:, m % 2], ACT.Tanh,
                                         scale=0.5).then_inc(tanh_done, 1)
                    act.wait_ge(dense_ready, base + n + 2)
                    for j in range(4):
                        col = 46 + 4 * kind + j
                        e = nc.scalar.activation(half_b[:, m % 2, j], dense_bank[(n + 1) % DENSE_BANKS][:, P * j:P * j + P],
                                                 ACT.Identity, scale=0.5, bias=bias_cols[:, col:col + 1])
                    e.then_inc(half_b_done, 1)
                    act.wait_ge(half_b_done, i * COUNT["up"] + m + 1)
                    act.sem_inc(dense_free[(n + 1) % DENSE_BANKS], 1)

            def dense_parts(i, t, more):
                for part in PLAN.get(t, ()):
                    dense_part(part, i, i * N_DENSE, i * (N_DENSE // DENSE_BANKS),
                               (DENSE if more else DENSE_LAST)[part])
                for part in AHEAD.get(t, ()) if more else ():
                    dense_part(part, i + 1, i * N_DENSE, i * (N_DENSE // DENSE_BANKS), DENSE[part])

            def body(i, more):
                for t in STEPS:
                    u = t - TURN_LAG
                    if 0 <= u < UNITS:
                        act.wait_ge(turned, i * UNITS + u + 1)
                        nc.scalar.copy(probs_t[:, u % 3].rearrange("p h t -> p (h t)"),
                                       turn_bank[u % TURN_BANKS][:]).then_inc(probs_t_ready, 1)
                    if 0 <= t < UNITS:
                        act.wait_ge(scored, i * UNITS + t + 1)
                        for h in range(QH):
                            e = nc.scalar.activation(probs[:, t % 4, h], score_bank[t % SCORE_BANKS][:, P * h:P * h + P],
                                                     ACT.Exp, bias=neg_max[:, t % 4, h:h + 1],
                                                     accum_out=row_sum[:, t % 4, h:h + 1])
                        e.then_inc(probs_ready, 1)
                    dense_parts(i, t, more)

            for t in sorted(AHEAD):
                for part in AHEAD[t]:
                    dense_part(part, 0, 0, 0, DENSE_FIRST[part])
            act.wait_ge(consts_ready, 2)
            act.wait_ge(setup_dve, 9)
            zero = one_cols[:, 0, D:D + 1]
            for r in range(FIRST + 2, RING):
                nc.scalar.copy(k_blocks[:, r].rearrange("p c h t -> p (c h t)"),
                               zero.broadcast_to([P, CK * HC * P])).then_inc(blocks_zeroed, 1)
            with act.Fori(0, ITERS - 1) as i:
                body(i, True)
            body(ITERS - 1, False)


        @block.vector
        def _(dve):
            dve.wait_ge(setup_act, 1)
            nc.vector.scalar_tensor_tensor(out=cond_silu, in0=cond_tanh, scalar=1.0, in1=cond,
                                           op0=ALU.add, op1=ALU.mult).then_inc(setup_dve, 1)
            dve.wait_ge(setup_dve, 1)
            nc.vector.tensor_scalar(cond_silu, cond_silu, 0.5, None, ALU.mult).then_inc(setup_dve, 1)
            dve.wait_ge(setup_pe, 1)
            nc.vector.tensor_copy(bias_cols[:], dense_bank[0][:, 0:NBIAS]).then_inc(setup_dve, 1)
            dve.wait_ge(setup_dve, 3)
            ada = bias_cols[:, 0:18].rearrange("p (k m) -> p k m", m=6)
            ss = bias_cols[:, 18:26].rearrange("p (k m) -> p k m", m=4)
            to_ada = mod_bias[:, 0:12].rearrange("p (k m) -> p k m", m=4)
            to_ss = mod_bias[:, 12:20].rearrange("p (k m) -> p k m", m=4)
            nc.vector.tensor_scalar(to_ada[:, :, 0:2], ada[:, :, 2:4], 1.0, None, ALU.add)
            nc.vector.tensor_scalar(to_ss[:, :, 0:2], ss[:, :, 0:2], 1.0, None, ALU.add)
            nc.vector.tensor_copy(to_ada[:, :, 2:4], ada[:, :, 0:2])
            nc.vector.tensor_copy(to_ss[:, :, 2:4], ss[:, :, 2:4])
            for kind in (SELF, CROSS, LAST):
                q = bias_cols[:, QUERY_BIAS[kind]:QUERY_BIAS[kind] + CK]
                nc.vector.tensor_scalar(q, q, 0.25, None, ALU.mult)
            nc.vector.tensor_scalar(bias_cols[:, 46:46 + HB], bias_cols[:, 46:46 + HB], 0.5, None,
                                    ALU.mult).then_inc(setup_dve, 1)
            dve.wait_ge(setup_pe, 2)
            nc.vector.tensor_copy(silu_t[:].rearrange("p c b -> p (c b)"),
                                  dense_bank[1][:, 0:CK * B]).then_inc(setup_dve, 1)
            dve.wait_ge(setup_pe, 3)
            mod_by_slot = mod_all[:].rearrange("p (i s) j -> p i s j", s=SLOTS)
            to_mod = mod_all[:].rearrange("p b j -> p j b")
            mod_psum = score_bank[0][:, 0:NMOD * B].rearrange("p (j b) -> p j b", b=B)
            nc.vector.tensor_tensor(to_mod[:, 0:4], mod_psum[:, 0:4], mod_bias[:, 0:4].unsqueeze(2).broadcast_to([P, 4, B]),
                                    ALU.add).then_inc(setup_dve, 1)
            dve.wait_ge(setup_dve, 6)
            for free in dense_free:
                dve.sem_inc(free, 1)
            dve.wait_ge(b_value_loaded, 3 * 16)

            def top_k(i, u):
                n = u - 4 * SLOTS
                bank_u, l = score_bank[u % SCORE_BANKS], left[:, u % 4]
                base = (i * 4 * SLOTS + n) * 4
                for h in range(QH):
                    e = nc.vector.max(top8[:, 0, h], bank_u[:, P * h:P * h + P])
                e.then_inc(topk_step, 1)
                dve.wait_ge(topk_step, base + 1)
                nc.vector.tensor_scalar(neg_max[:, u % 4].unsqueeze(2), top8[:, 0, :, 0:1], -1.0, None,
                                        ALU.mult)
                for h in range(QH):
                    e = nc.vector.match_replace(l[:, h], top8[:, 0, h], bank_u[:, P * h:P * h + P], GONE)
                e.then_inc(topk_step, 1)
                dve.wait_ge(topk_step, base + 2)
                dve.sem_inc(scored, 1)
                for h in range(QH):
                    e = nc.vector.max(top8[:, 1, h], l[:, h])
                e.then_inc(topk_step, 1)
                dve.wait_ge(topk_step, base + 3)
                dve.sem_inc(dve_passed, 1)
                for h in range(QH):
                    e = nc.vector.match_replace(l[:, h], top8[:, 1, h], l[:, h], GONE)
                    if h == 0:
                        e.then_inc(topk_step, 1)
                e.then_inc(left_ready, 1)

            def dense_part(part, i, base, round_, n_dense):
                name, kind, s = part
                n, m = n_dense, NTH[part]
                d = dense_bank[n % DENSE_BANKS]
                if name == "stats":
                    src = {SELF: x_in, CTX: ctx_in}.get(kind, x_mid)[:, s, :]
                    if kind == SELF:
                        nc.vector.tensor_copy(mod_now[:, s, 0:4], mod_by_slot[:, i, s, 0:4]).then_inc(mod_ready, 1)
                        dve.wait_ge(x_loaded[s], (i + 1) * 16)
                    elif kind == CTX:
                        nc.vector.tensor_copy(mod_now[:, s, 4:], mod_by_slot[:, i, s, 4:]).then_inc(mod_rest_ready, 1)
                        dve.wait_ge(ctx_loaded[s], (i + 1) * 16)
                    else:
                        before = {CROSS: SELF, MLP: CROSS, LAST: MLP}[kind]
                        dve.wait_ge(x_done, i * N_OUT + NTH["out", before, s] + 1)
                    nc.vector.bn_stats(ln_stats[:, m % 4], src).then_inc(bn_done, 1)
                    dve.wait_ge(bn_done, i * COUNT["stats"] + m + 1)
                    dve.sem_inc(dve_passed, 1)
                    nc.vector.bn_aggr(ln_mv[:, m % 4], ln_stats[:, m % 4]).then_inc(stats_done, 1)
                if name == "norm":
                    src = {SELF: x_in, CTX: ctx_in}.get(kind, x_mid)[:, s, :]
                    dve.wait_ge(rstd_done, i * COUNT["stats"] + NTH["stats", kind, s] + 1)
                    g = NTH["stats", kind, s] % 4
                    nc.vector.tensor_scalar(x_norm[:, m % 3], src, ln_mv[:, g, 0:1], ln_rstd[:, g, 0:1],
                                            ALU.subtract, ALU.mult).then_inc(norm_done, 1)
                if name == "q":
                    r = phase_of(kind, s) % RING
                    b = bias_cols[:, QUERY_BIAS[kind]:QUERY_BIAS[kind] + CK]
                    dve.wait_ge(dense_ready, base + n + 1)
                    nc.vector.tensor_tensor(q_t[:, r], d[:, 0:C].rearrange("p (c t) -> p c t", t=P),
                                            b.unsqueeze(2).broadcast_to([P, CK, P]), ALU.add).then_inc(q_ready, 1)
                    dve.wait_ge(q_ready, i * COUNT["q"] + m + 1)
                    dve.sem_inc(dense_free[n % DENSE_BANKS], 1)
                if name == "kv":
                    r = phase_of(kind, s) % RING
                    b = bias_cols[:, KEY_BIAS[kind]:KEY_BIAS[kind] + CK]
                    if m >= 3:
                        old = phase_of(*KV_ORDER[m - 3])
                        dve.wait_ge(k_placed[old % RING], i * FILLS * 16 * HC + 16 * HC * (old // RING + 1))
                    dve.wait_ge(dense_ready, base + n + 1)
                    nc.vector.tensor_tensor(k_t[:, m % 3], d[:, 0:C].rearrange("p (c t) -> p c t", t=P),
                                            b.unsqueeze(2).broadcast_to([P, CK, P]), ALU.add).then_inc(k_ready, 1)
                    v = v_pad[:, r].rearrange("p g a j -> p (g a j)").rearrange("p (g w) -> p g w", w=64)
                    for odd in range(2):
                        src = d[:, C:2 * C].rearrange("p (g a j) -> p g a j", a=2, j=D)[:, :, odd]
                        bv = b_value[:, kind].rearrange("p (g a j) -> p g a j", a=2, j=D)[:, :, odd]
                        e = nc.vector.tensor_tensor(v[:, :, 48 * odd:48 * odd + D], src, bv, ALU.add)
                    e.then_inc(v_ready, 1)
                    dve.wait_ge(v_ready, i * COUNT["kv"] + m + 1)
                    dve.sem_inc(dense_free[n % DENSE_BANKS], 1)
                if name == "out":
                    dve.wait_ge(dense_ready, base + n + 1)
                    skip = i * COUNT["skip"] + NTH["skip", kind, s] + 1
                    if kind == LAST:
                        dve.wait_ge(skip_ready, skip)
                        nc.vector.tensor_tensor(x_mid[:, s, :], d[:, 0:C], x_skip[:, s, :],
                                                ALU.add).then_inc(x_done, 1)
                        dve.wait_ge(x_done, i * N_OUT + m + 1)
                        dve.sem_inc(dense_free[n % DENSE_BANKS], 1)
                    else:
                        g = gates[:, s, GATE[kind] * C:(GATE[kind] + 1) * C]
                        dve.wait_ge(gates_loaded[s], (i + 1) * 16)
                        nc.vector.tensor_tensor(gated[:], d[:, 0:C], g, ALU.mult).then_inc(dense_free[n % DENSE_BANKS], 1)
                        dve.wait_ge(dense_free[n % DENSE_BANKS], round_ + n // DENSE_BANKS + 2)
                        dve.wait_ge(skip_ready, skip)
                        if kind == SELF:
                            dve.wait_ge(y_gone, i + 1)
                        nc.vector.tensor_tensor(x_mid[:, s, :], gated[:], x_skip[:, s, :],
                                                ALU.add).then_inc(x_done, 1)
                if name == "up":
                    dve.wait_ge(dense_ready, base + n + 1)
                    b = bias_cols[:, 38 + 4 * kind:42 + 4 * kind]
                    nc.vector.tensor_tensor(lin_a[:, m % 2], d[:].rearrange("p (j t) -> p j t", t=P),
                                            b.unsqueeze(2).broadcast_to([P, 4, P]), ALU.add).then_inc(lin_a_done, 1)
                    dve.wait_ge(lin_a_done, i * COUNT["up"] + m + 1)
                    dve.sem_inc(dense_free[n % DENSE_BANKS], 1)
                if name == "glu":
                    dve.wait_ge(tanh_done, i * COUNT["glu"] + m + 1)
                    nc.vector.scalar_tensor_tensor(
                        out=tanh_a[:, m % 2].rearrange("p j t -> p (j t)"),
                        in0=tanh_a[:, m % 2].rearrange("p j t -> p (j t)"), scalar=1.0,
                        in1=lin_a[:, m % 2].rearrange("p j t -> p (j t)"),
                        op0=ALU.add, op1=ALU.mult).then_inc(silu_done, 1)

            def dense_parts(i, t, more, when):
                for part in PLAN.get(t, ()):
                    if dve_order(part) == when:
                        dense_part(part, i, i * N_DENSE, i * (N_DENSE // DENSE_BANKS),
                                   (DENSE if more else DENSE_LAST)[part])
                for part in AHEAD.get(t, ()) if more else ():
                    if dve_order(part) == when:
                        dense_part(part, i + 1, i * N_DENSE, i * (N_DENSE // DENSE_BANKS), DENSE[part])

            def body(i, more):
                for t in STEPS:
                    dense_parts(i, t, more, EARLY)
                    u = t - O_LAG
                    if 0 <= u < UNITS and u % 4 == 3:
                        ph = u // 4
                        dve.wait_ge(o_ready, i * PHASES + ph + 1)
                        if ph // SLOTS == CROSS:
                            nc.vector.reciprocal(inv_sum[:], o_view[:, :, 1]).then_inc(inv_done, 1)
                            dve.wait_ge(inv_done, i * SLOTS + ph % SLOTS + 1)
                            nc.vector.tensor_tensor(o_t[:], o_view[:, :, 0], inv_sum[:], ALU.mult).then_inc(o_t_ready, 1)
                        else:
                            nc.vector.tensor_copy(o_t[:], o_view[:, :, 0]).then_inc(o_t_ready, 1)
                    if 0 <= t < UNITS:
                        dve.wait_ge(scores_ready, i * UNITS + t + 1)
                        dve.sem_inc(dve_passed, 1)
                        if t // (4 * SLOTS) == CROSS:
                            top_k(i, t)
                        else:
                            nc.vector.tensor_reduce(neg_max[:, t % 4], score_bank[t % SCORE_BANKS][:].rearrange("p (h t) -> p h t", t=P),
                                                    AX.X, ALU.max, negate=True).then_inc(scored, 1)
                    dense_parts(i, t - 1, more, LATE)
                    u = t - 1
                    if 0 <= u < UNITS and u // (4 * SLOTS) != CROSS:
                        dve.wait_ge(probs_ready, i * UNITS + u + 1)
                        nc.vector.reciprocal(row_sum[:, u % 4], row_sum[:, u % 4]).then_inc(inv_row_done, 1)
                    dense_parts(i, t, more, ON_TIME)

            for t in sorted(AHEAD):
                for part in AHEAD[t]:
                    dense_part(part, 0, 0, 0, DENSE_FIRST[part])
            dve.wait_ge(setup_pe, 4)
            nc.vector.tensor_tensor(to_mod[:, 4:], mod_psum[:, 4:], mod_bias[:, 4:].unsqueeze(2).broadcast_to([P, NMOD - 4, B]),
                                    ALU.add).then_inc(setup_dve, 1)
            dve.wait_ge(gate_bias_loaded, 16)
            dve.wait_ge(setup_pe, 5)
            nc.vector.tensor_tensor(gate_rows[:, 0:2 * C], score_bank[1][0:B, :], gate_bias[:, 0:2 * C],
                                    ALU.add).then_inc(setup_dve, 1)
            nc.vector.tensor_tensor(gate_rows[:, 2 * C:3 * C], score_bank[2][0:B, 0:C], gate_bias[:, 2 * C:3 * C],
                                    ALU.add).then_inc(setup_dve, 1)
            dve.wait_ge(setup_dve, 9)
            with dve.Fori(0, ITERS - 1) as i:
                body(i, True)
            body(ITERS - 1, False)


        @block.tensor
        def _(pe):
            pe.wait_ge(consts_ready, 1)
            pe.wait_ge(rows_loaded, 9 * 16)
            nc.tensor.transpose(dense_bank[0][:, 0:NBIAS], bias_rows[:], ident[0:NBIAS, 0:NBIAS]).then_inc(setup_pe, 1)
            pe.wait_ge(setup_dve, 2)
            for c in range(CK):
                e = nc.tensor.transpose(dense_bank[1][:, B * c:B * c + B], cond_silu[:, P * c:P * c + P], ident[0:B, 0:B])
            e.then_inc(setup_pe, 1)
            pe.wait_ge(setup_dve, 5)

            def modulate(first, w):
                for j, block_w in enumerate(w, first):
                    for c in range(CK):
                        e = nc.tensor.matmul(score_bank[0][:, B * j:B * j + B], block_w[:, c], silu_t[:, c],
                                             start=(c == 0), stop=(c == CK - 1))
                return e

            def ada_blocks(k):
                return [w_ada[:, :, C * m + P * c:C * m + P * c + P] for m in (3 * k + 1, 3 * k) for c in range(CK)]

            pe.wait_ge(ada_loaded[0], 16)
            modulate(0, ada_blocks(0)).then_inc(setup_pe, 1)
            pe.wait_ge(w_loaded["qkv"], 16)
            pe.wait_ge(w_scaled, 1)

            def dense_part(part, i, base, round_, n_dense):
                name, kind, s = part
                if s == 0:
                    for key in WEIGHTS.get((name, kind), ()):
                        pe.wait_ge(w_loaded[key], 16)
                    if (name, kind) in SCALED:
                        pe.wait_ge(w_scaled, SCALED[name, kind])
                n = n_dense
                d = dense_bank[n % DENSE_BANKS]
                if name in DENSE_USES:
                    pe.wait_ge(dense_free[n % DENSE_BANKS], round_ + n // DENSE_BANKS + 1)
                if name == "turn":
                    pe.wait_ge(norm_done, i * COUNT["norm"] + NTH["norm", kind, s] + 1)
                    g = NTH["norm", kind, s] % 3
                    for c in range(CK):
                        e = nc.tensor.transpose(d[:, P * c:P * c + P], x_norm[:, g, P * c:P * c + P], ident[:])
                    e.then_inc(dense_ready, 1)
                if name == "turn_ctx":
                    pe.wait_ge(norm_done, i * COUNT["norm"] + NTH["norm", kind, s] + 1)
                    g = NTH["norm", kind, s] % 3
                    for c in range(CK):
                        nc.tensor.transpose(d[:, P * c:P * c + P], ctx_in[:, s, P * c:P * c + P], ident[:])
                    for c in range(CK):
                        e = nc.tensor.transpose(d[:, P * (2 + c):P * (3 + c)], x_norm[:, g, P * c:P * c + P], ident[:])
                    e.then_inc(dense_ready, 1)
                if name == "q":
                    pe.wait_ge(h_ready, (i * COUNT["turn"] + NTH["turn", kind, s] + 1) * 2)
                    for j in range(CK):
                        for c in range(CK):
                            e = nc.tensor.matmul(d[:, P * j:P * j + P], w_query[kind][:, c, P * j:P * j + P],
                                                 h_t[:, s, c], start=(c == 0), stop=(c == CK - 1))
                    e.then_inc(dense_ready, 1)
                if name == "kv":
                    src = {SELF: h_t[:, s], CROSS: ctx_t[:, 0], LAST: ctx_norm_t[:, s % 3]}[kind]
                    turn = ("turn", SELF, s) if kind == SELF else ("turn_ctx", CTX, s)
                    pe.wait_ge(h_ready, (i * COUNT["turn"] + NTH[turn] + 1) * 2)
                    for j in range(CK):
                        for c in range(CK):
                            nc.tensor.matmul(d[:, P * j:P * j + P], w_key[kind][:, c, P * j:P * j + P],
                                             src[:, c], start=(c == 0), stop=(c == CK - 1))
                    for c in range(CK):
                        e = nc.tensor.matmul(d[:, C:2 * C], src[:, c], w_value[kind][:, c],
                                             start=(c == 0), stop=(c == CK - 1))
                    e.then_inc(dense_ready, 1)
                if name == "out" and kind != MLP:
                    pe.wait_ge(o_t_ready, i * PHASES + phase_of(kind, s) + 1)
                    for c in range(CK):
                        e = nc.tensor.matmul(d[:, 0:C], o_t[:, c], w_out[kind][:, c],
                                             start=(c == 0), stop=(c == CK - 1))
                    e.then_inc(dense_ready, 1)
                if name == "up":
                    if kind == 0:
                        pe.wait_ge(h_ready, (i * COUNT["turn"] + NTH["turn", MLP, s] + 1) * 2)
                    for lin in range(2):
                        d = dense_bank[(n + lin) % DENSE_BANKS]
                        if lin:
                            pe.wait_ge(dense_free[(n + 1) % DENSE_BANKS], round_ + (n + 1) // DENSE_BANKS + 1)
                        for j in range(4):
                            at = HID * lin + P * (4 * kind + j)
                            for c in range(CK):
                                e = nc.tensor.matmul(d[:, P * j:P * j + P], w_m1[:, c, at:at + P], h_t[:, s, c],
                                                     start=(c == 0), stop=(c == CK - 1))
                        e.then_inc(dense_ready, 1)
                if name == "out" and kind == MLP:
                    for j in range(HB):
                        if j % 4 == 0:
                            pe.wait_ge(glu_done, i * COUNT["glu"] + NTH["glu", j // 4, s] + 1)
                        e = nc.tensor.matmul(d[:, 0:C], glu[:, j], w_m2[:, j],
                                             start=(j == 0), stop=(j == HB - 1))
                    e.then_inc(dense_ready, 1)

            def dense_parts(i, t, more):
                for part in PLAN.get(t, ()):
                    dense_part(part, i, i * N_DENSE, i * (N_DENSE // DENSE_BANKS),
                               (DENSE if more else DENSE_LAST)[part])
                for part in AHEAD.get(t, ()) if more else ():
                    dense_part(part, i + 1, i * N_DENSE, i * (N_DENSE // DENSE_BANKS), DENSE[part])

            def body(i, more):
                for t in STEPS:
                    u = t - TURN_LAG
                    if 0 <= u < UNITS:
                        pe.wait_ge(weights_ready, i * UNITS + u + 1)
                        src = left if u // (4 * SLOTS) == CROSS else probs
                        if u >= TURN_BANKS:
                            pe.wait_ge(probs_t_ready, i * UNITS + u - TURN_BANKS + 1)
                        for h in range(QH):
                            e = nc.tensor.transpose(turn_bank[u % TURN_BANKS][:, P * h:P * h + P], src[:, u % 4, h], ident[:])
                        e.then_inc(turned, 1)
                    u = t + SCORE_AHEAD
                    if 0 <= u < UNITS:
                        ph, c, blk = u // 4, u % 4 // 2, 4 * (u % 2)
                        kind, s, r = ph // SLOTS, ph % SLOTS, ph % RING
                        if u % 4 == 0:
                            pe.wait_ge(q_ready, i * COUNT["q"] + NTH["q", kind, s] + 1)
                            pe.wait_ge(k_placed[r], i * FILLS * 16 * HC + 16 * HC * (ph // RING + 1))
                        if u >= SCORE_BANKS:
                            pe.wait_ge(probs_ready, i * UNITS + u - SCORE_BANKS + 1)
                        nc.tensor.matmul(score_bank[u % SCORE_BANKS][:], q_t[:, r, c],
                                         k_blocks[:, r, c, blk:blk + 4].rearrange("p h t -> p (h t)"),
                                         start=True, stop=True).then_inc(scores_ready, 1)
                    u = t - SUM_LAG
                    if 0 <= u < UNITS:
                        ph, c = u // 4, u % 4 // 2
                        kind, s, r = ph // SLOTS, ph % SLOTS, ph % RING
                        if u % 4 == 0:
                            pe.wait_ge(v_ready, i * COUNT["kv"] + NTH["kv", kind, s] + 1)
                            if ph:
                                pe.wait_ge(o_t_ready, i * PHASES + ph)
                        pe.wait_ge(probs_t_ready, i * UNITS + u + 1)
                        for what in range(2 if kind == CROSS else 1):
                            for g in range(2):
                                lane = 32 * (2 * (u % 2) + g)
                                for odd in range(2):
                                    w = v_pad[:, r, 2 * (u % 4) + g, odd] if what == 0 else one_cols[:, odd]
                                    e = nc.tensor.matmul(o_view[lane:lane + 32, c, what], w, probs_t[:, u % 3, 2 * g + odd],
                                                         start=(odd == 0), stop=(odd == 1))
                        if u % 4 == 3:
                            e.then_inc(o_ready, 1)
                    dense_parts(i, t, more)

            for t in sorted(AHEAD):
                for part in AHEAD[t]:
                    if part == ("turn", SELF, 1):
                        for k in range(1, 3):
                            pe.wait_ge(ada_loaded[k], 16)
                            modulate(4 * k, ada_blocks(k))
                    dense_part(part, 0, 0, 0, DENSE_FIRST[part])
            pe.wait_ge(ss_loaded, 2 * 16)
            modulate(12, [w[:, :, P * c:P * c + P] for w in (ss_q, ss_kv) for c in range(4)]).then_inc(setup_pe, 1)
            for k in range(3):
                dst = score_bank[1][0:B, C * k:C * k + C] if k < 2 else score_bank[2][0:B, 0:C]
                for c in range(CK):
                    e = nc.tensor.matmul(dst, silu_t[:, c], w_ada[:, c, C * (3 * k + 2):C * (3 * k + 3)],
                                         start=(c == 0), stop=(c == CK - 1))
            e.then_inc(setup_pe, 1)
            pe.wait_ge(consts_ready, 2)
            pe.wait_ge(setup_dve, 9)
            with pe.Fori(0, ITERS - 1) as i:
                body(i, True)
            body(ITERS - 1, False)



PLAN_SKIPS_LAST = [NTH["skip", LAST, s] for s in range(SLOTS)]

_INS = ["x", "cond_1024", "ctx_1024", "L0_xcond_w_ada", "L0_xcond_b_ada", "L0_xcond_w_qkv", "L0_xcond_b_qkv",
        "L0_xcond_w_so", "L0_xcond_b_so", "L0_xcond_w_q", "L0_xcond_b_q", "L0_xcond_w_kv", "L0_xcond_b_kv",
        "L0_xcond_w_co", "L0_xcond_b_co", "L0_xcond_w_m1", "L0_xcond_b_m1", "L0_xcond_w_m2", "L0_xcond_b_m2",
        "L1_xcond_Wq", "L1_xcond_bq", "L1_xcond_Wkv", "L1_xcond_bkv", "L1_xcond_Wp", "L1_xcond_bp",
        "L1_xcond_Wss_q", "L1_xcond_bss_q", "L1_xcond_Wss_kv", "L1_xcond_bss_kv"]


def kernel(**inputs):
    import numpy as np
    import concourse.bacc as bacc
    from concourse import mybir as _mybir
    from concourse.bass_utils import run_bass_kernel_spmd

    nc = bacc.Bacc("TRN2", target_bir_lowering=False, num_devices=1)
    arrays, aps = {}, {}
    for name in _INS:
        arr = np.ascontiguousarray(inputs[name])
        arrays[f"in_{name}"] = arr
        aps[name] = nc.dram_tensor(f"in_{name}", arr.shape, _mybir.dt.from_np(arr.dtype), kind="ExternalInput").ap()
    out = nc.dram_tensor("out_y", (B, P, C), F32, kind="ExternalOutput").ap()
    block_kernel(nc, aps, out)
    r = run_bass_kernel_spmd(nc, [arrays], core_ids=[0])
    return r.results[0]["out_y"]
```
